# Optimizing a Trainium2 kernel written in Bass

```python
import numpy as np
import jax
import jax.numpy as jnp

def _softmax(x, axis=-1):
    return jax.nn.softmax(x, axis=axis)

def _gelu(x):
    return jax.nn.gelu(x, approximate=True)

def _silu(x):
    return jax.nn.silu(x)

def _sigmoid(x):
    return jax.nn.sigmoid(x)

def _layernorm(x, axis=-1, eps=1e-05):
    m = jnp.mean(x, axis=axis, keepdims=True)
    v = jnp.var(x, axis=axis, keepdims=True)
    return (x - m) / jnp.sqrt(v + eps)

def _scatter_add(tgt, idx, src, axis=0):
    return tgt.at[idx].add(src)

def _segment_sum(src, seg, n):
    return jax.ops.segment_sum(src, seg, n)
kernel_name = 'mk_adj_resnorm_d2_adj_r2_b500aa'

def setup_inputs(seed: int=0):
    np.random.seed(seed)
    _w = jnp.asarray

    def _rec_inputs():
        import jax
        import jax.numpy as jnp
        _gk = jax.random.key(seed)
        x = -0.001003 + 1 * jax.random.normal(jax.random.fold_in(_gk, 1), (4096, 256), jnp.float32)
        _a = jax.random.bernoulli(jax.random.fold_in(_gk, 2), 0.00195312, (4096, 4096))
        _a = jnp.logical_or(_a, jnp.swapaxes(_a, -1, -2))
        _a = jnp.logical_or(_a, jnp.eye(4096, dtype=bool))
        _af = _a.astype(jnp.float32)
        adj = _af
        return (x, adj)
    x, adj = _rec_inputs()

    def _L0_gnn_setup():
        import jax, jax.numpy as jnp
        import numpy as np
        N, F, H = (1536, 256, 4)
        D = F // H
        ALPHA = 0.5
        EPS = 1e-06

        def _batchnorm(x, gamma, beta):
            m = jnp.mean(x, axis=0)
            v = jnp.var(x, axis=0)
            return (x - m) * jax.lax.rsqrt(v + EPS) * gamma + beta

        def _masked_softmax(scores, mask):
            s = jnp.where(mask, scores, -jnp.inf)
            att = jax.nn.softmax(s, axis=-1)
            return jnp.where(mask, att, 0.0)

        def _mlp_block(x, Wm, bm, g, b):
            h = jax.nn.elu(x @ Wm.T + bm) + x
            return _batchnorm(h, g, b)
        key = jax.random.key(seed)
        ks = jax.random.split(key, 12)
        X = jax.random.normal(ks[0], (N, F), dtype=jnp.float32)
        eye = jnp.eye(N, dtype=jnp.float32)
        local = (jax.random.uniform(ks[1], (N, N)) < 32.0 / N).astype(jnp.float32)
        local = jnp.clip(local + eye, 0.0, 1.0)
        longr = (jax.random.uniform(ks[2], (N, N)) < 16.0 / N).astype(jnp.float32)
        longr = jnp.clip(longr + eye, 0.0, 1.0)
        W = jax.random.normal(ks[3], (H, D, D), dtype=jnp.float32) * 0.1
        V = jax.random.normal(ks[4], (H, 2, D, 1), dtype=jnp.float32) * 0.1
        return {'X': X, 'local_pattern': local, 'long_range_pattern': longr, 'W': W, 'V': V, 'enc_bn_gamma': jnp.ones((F,), jnp.float32), 'enc_bn_beta': jnp.zeros((F,), jnp.float32), 'enc_mlp_W': jax.random.normal(ks[5], (F, F), dtype=jnp.float32) * 0.02, 'enc_mlp_b': jnp.zeros((F,), jnp.float32), 'enc_mlp_bn_gamma': jnp.ones((F,), jnp.float32), 'enc_mlp_bn_beta': jnp.zeros((F,), jnp.float32), 'dec_mlp_W': jax.random.normal(ks[6], (F, F), dtype=jnp.float32) * 0.02, 'dec_mlp_b': jnp.zeros((F,), jnp.float32), 'dec_mlp_bn_gamma': jnp.ones((F,), jnp.float32), 'dec_mlp_bn_beta': jnp.zeros((F,), jnp.float32)}
    _L0_gnn_all = _L0_gnn_setup()
    _L0_gnn_in = {k: v for k, v in _L0_gnn_all.items() if k in ('W', 'V', 'enc_bn_gamma', 'enc_bn_beta', 'enc_mlp_W', 'enc_mlp_b', 'enc_mlp_bn_gamma', 'enc_mlp_bn_beta', 'dec_mlp_W', 'dec_mlp_b', 'dec_mlp_bn_gamma', 'dec_mlp_bn_beta')}
    del _L0_gnn_all

    def _L1_gnn_setup():
        import jax, jax.numpy as jnp
        import numpy as np
        N = 4096
        D = 256
        EPS = 1e-12
        key = jax.random.key(seed)
        k1, k2 = jax.random.split(key)
        cur = jax.random.normal(k1, (N, D), dtype=jnp.float32)
        incidence_m = jax.random.normal(k2, (N, N), dtype=jnp.float32)
        return {'cur': cur, 'incidence_m': incidence_m}
    _L1_gnn_all = _L1_gnn_setup()
    _L1_gnn_in = {k: v for k, v in _L1_gnn_all.items() if k in ()}
    del _L1_gnn_all
    return {'x': x, 'adj': adj, 'L0_gnn_W': _L0_gnn_in['W'], 'L0_gnn_V': _L0_gnn_in['V'], 'L0_gnn_enc_bn_gamma': _L0_gnn_in['enc_bn_gamma'], 'L0_gnn_enc_bn_beta': _L0_gnn_in['enc_bn_beta'], 'L0_gnn_enc_mlp_W': _L0_gnn_in['enc_mlp_W'], 'L0_gnn_enc_mlp_b': _L0_gnn_in['enc_mlp_b'], 'L0_gnn_enc_mlp_bn_gamma': _L0_gnn_in['enc_mlp_bn_gamma'], 'L0_gnn_enc_mlp_bn_beta': _L0_gnn_in['enc_mlp_bn_beta'], 'L0_gnn_dec_mlp_W': _L0_gnn_in['dec_mlp_W'], 'L0_gnn_dec_mlp_b': _L0_gnn_in['dec_mlp_b'], 'L0_gnn_dec_mlp_bn_gamma': _L0_gnn_in['dec_mlp_bn_gamma'], 'L0_gnn_dec_mlp_bn_beta': _L0_gnn_in['dec_mlp_bn_beta']}

def reference(x, adj, L0_gnn_W, L0_gnn_V, L0_gnn_enc_bn_gamma, L0_gnn_enc_bn_beta, L0_gnn_enc_mlp_W, L0_gnn_enc_mlp_b, L0_gnn_enc_mlp_bn_gamma, L0_gnn_enc_mlp_bn_beta, L0_gnn_dec_mlp_W, L0_gnn_dec_mlp_b, L0_gnn_dec_mlp_bn_gamma, L0_gnn_dec_mlp_bn_beta):
    import jax
    import jax.numpy as jnp

    def _L0_gnn_ref(X, local_pattern, long_range_pattern, W, V, enc_bn_gamma, enc_bn_beta, enc_mlp_W, enc_mlp_b, enc_mlp_bn_gamma, enc_mlp_bn_beta, dec_mlp_W, dec_mlp_b, dec_mlp_bn_gamma, dec_mlp_bn_beta):
        import jax, jax.numpy as jnp
        import numpy as np
        N, F, H = (1536, 256, 4)
        D = F // H
        ALPHA = 0.5
        EPS = 1e-06

        def _batchnorm(x, gamma, beta):
            m = jnp.mean(x, axis=0)
            v = jnp.var(x, axis=0)
            return (x - m) * jax.lax.rsqrt(v + EPS) * gamma + beta

        def _masked_softmax(scores, mask):
            s = jnp.where(mask, scores, -jnp.inf)
            att = jax.nn.softmax(s, axis=-1)
            return jnp.where(mask, att, 0.0)

        def _mlp_block(x, Wm, bm, g, b):
            h = jax.nn.elu(x @ Wm.T + bm) + x
            return _batchnorm(h, g, b)
        n = X.shape[0]
        Xh = X.reshape(n, H, D).transpose(1, 0, 2)
        Xw = jnp.einsum('hnd,hde->hne', Xh, W)
        f1 = jnp.einsum('hnd,hd->hn', Xw, V[:, 0, :, 0])
        f2 = jnp.einsum('hnd,hd->hn', Xw, V[:, 1, :, 0])
        sig = jax.nn.sigmoid(f1[:, :, None] + f2[:, None, :])
        lmask = (local_pattern != 0)[None]
        gmask = (long_range_pattern != 0)[None]
        local_att = _masked_softmax(local_pattern[None] * sig, lmask)
        long_att = _masked_softmax(long_range_pattern[None] * sig, gmask)
        att = ALPHA * long_att + (1.0 - ALPHA) * local_att
        Xa = jnp.einsum('hij,hjd->hid', att, Xw)
        Xc = Xa.transpose(1, 0, 2).reshape(n, F)
        Xn = _batchnorm(Xc, enc_bn_gamma, enc_bn_beta)
        emb = _mlp_block(Xn, enc_mlp_W, enc_mlp_b, enc_mlp_bn_gamma, enc_mlp_bn_beta)
        Yh = emb.reshape(n, H, D).transpose(1, 0, 2)
        Y = jnp.einsum('hij,hjd->hid', att, Yh)
        Y = jnp.einsum('hnd,hed->hne', Y, W)
        Yc = Y.transpose(1, 0, 2).reshape(n, F)
        Yc = jax.nn.elu(Yc)
        out = _mlp_block(Yc, dec_mlp_W, dec_mlp_b, dec_mlp_bn_gamma, dec_mlp_bn_beta)
        return out

    def _L1_gnn_ref(cur, incidence_m):
        import jax, jax.numpy as jnp
        import numpy as np
        N = 4096
        D = 256
        EPS = 1e-12
        mask = incidence_m > 0
        head = jax.lax.stop_gradient(mask.astype(incidence_m.dtype))
        head = head / jnp.maximum(jnp.sqrt(jnp.sum(head * head, axis=-1, keepdims=True)), EPS)
        inc = incidence_m + head
        edge_fea = inc @ cur
        edge_degree = jnp.sum(inc, axis=-1, keepdims=True)
        return edge_fea / edge_degree
    x = _layernorm(x + _L0_gnn_ref(x, adj, adj, L0_gnn_W, L0_gnn_V, L0_gnn_enc_bn_gamma, L0_gnn_enc_bn_beta, L0_gnn_enc_mlp_W, L0_gnn_enc_mlp_b, L0_gnn_enc_mlp_bn_gamma, L0_gnn_enc_mlp_bn_beta, L0_gnn_dec_mlp_W, L0_gnn_dec_mlp_b, L0_gnn_dec_mlp_bn_gamma, L0_gnn_dec_mlp_bn_beta), axis=-1)
    x = _layernorm(x + _L1_gnn_ref(x, adj), axis=-1)
    return x

_drawn_inputs = setup_inputs


def setup_inputs(seed=0):
    import zlib

    import numpy as np

    out = dict(_drawn_inputs(seed))
    spreads = {'L0_gnn_enc_bn_gamma': (1.0, 0.2),
     'L0_gnn_enc_bn_beta': (0.0, 0.8),
     'L0_gnn_enc_mlp_b': (0.0, 0.8),
     'L0_gnn_enc_mlp_bn_gamma': (1.0, 0.2),
     'L0_gnn_enc_mlp_bn_beta': (0.0, 0.514),
     'L0_gnn_dec_mlp_b': (0.0, 0.776),
     'L0_gnn_dec_mlp_bn_gamma': (1.0, 0.2),
     'L0_gnn_dec_mlp_bn_beta': (0.0, 0.1)}
    factors = {}
    for name, (base, spread) in spreads.items():
        noise = np.random.default_rng([zlib.crc32(name.encode()), seed]).standard_normal(out[name].shape)
        drawn = base * np.exp(spread * noise) if base else spread * noise
        out[name] = jnp.asarray(drawn.astype(out[name].dtype))
    for name, factor in factors.items():
        out[name] = (out[name] * factor).astype(out[name].dtype)
    return out
```

```python
from contextlib import ExitStack

import concourse.bass as bass
from concourse import mybir

ALU = mybir.AluOpType
ACT = mybir.ActivationFunctionType
F32 = mybir.dt.float32
F16 = mybir.dt.float16
F8 = mybir.dt.float8e4
ds = bass.ds

P = 128
N = 4096
F = 256
H = 4
D = F // H
NT = N // P
NB = F // P
HP = 2
CH = 2048
NCH = N // CH
BK = 512
NC = N // BK
PASSES = NCH * NB
RING = 4
ITS = NT // RING
EPS_BN = 1e-6
EPS_LN = 1e-5
EPS_NORM = 1e-12
TINY = 1e-30
LO_SCALE = 2048.0
GI = 512
NG = N // GI
GT = GI // P


def build(nc, xT, x, adjT, W, WT, V, enc_g, enc_b, encm_WT, encm_bias, encm_g, encm_b,
          decm_WT, decm_bias, decm_g, decm_b, out):
    adj8 = nc.dram_tensor("adj8", [N, N // 4], F32, kind="Internal").ap()
    f1_d = nc.dram_tensor("f1_d", [H, N], F32, kind="Internal").ap()
    den_d = nc.dram_tensor("den_d", [H, N], F32, kind="Internal").ap()
    rec_d = nc.dram_tensor("rec_d", [H, N], F32, kind="Internal").ap()

    with ExitStack() as ctx:
        def sb(name, shape, dt=F32):
            return ctx.enter_context(nc.sbuf_tensor(name, shape, dt))

        def sem(name):
            return ctx.enter_context(nc.semaphore(name))

        vals = sb("vals", [P, NT, F])
        agg = sb("agg", [P, NB, N])
        ering = sb("ering", [P, RING, HP * CH])
        f1b = sb("f1b", [P, 2, HP, CH])
        io = sb("io", [P, 8192])
        vx = sb("vx", [P, RING, HP, D + 1])
        wm = sb("wm", [P, NB, P + 2 * H])
        wtbd = sb("wtbd", [P, NB, P])
        vbd = sb("vbd", [P, NB, 2 * H])
        wenc = sb("wenc", [P, NB, F])
        wdec = sb("wdec", [P, NB, F])
        cols = sb("cols", [P, NB, 8])
        f2h = sb("f2h", [P, NT, H])
        dsm = sb("dsm", [P, 32])
        rsm = sb("rsm", [P, 32])
        ident = sb("ident", [P, P])
        ones16 = sb("ones16", [P, 2], F16)
        eps = sb("eps", [P, 2])
        stats = sb("stats", [P, NB, NC, 6])
        mv = sb("mv", [P, NB, 2])
        bnc = sb("bnc", [P, NB, 4])
        lnst = sb("lnst", [P, NT, 6])
        lnmv = sb("lnmv", [P, NT, 2])
        lnsd = sb("lnsd", [P, NT, 2])
        degs = sb("degs", [P, GT, 8])
        ps = ctx.enter_context(nc.psum_tensor("ps", [P, 8, BK], F32))

        mask_w = io[:, 0:RING * CH // 4].rearrange("p (s n) -> p s n", s=RING)
        mask = io[:, 0:RING * CH // 4].bitcast(F8).rearrange("p (s n) -> p s n", s=RING)
        stage = io[:, 2048:6144].rearrange("p (s n) -> p s n", s=2)
        rden = io[:, 6144:8192]
        adjg_w = io[:, :].rearrange("p (s t n) -> p s t n", s=2, t=NT)
        adjg = io[:, :].bitcast(F8).rearrange("p (s t n) -> p s t n", s=2, t=NT)
        xTs = ering[:, 0:2, :]
        f1row = agg[0:H, 0, :]
        h_enc = ering[:, 0:2, :]
        tmp_enc = ering[:, 2:4, :].rearrange("p a (k n) -> p a k n", n=BK)
        yc = ering[:, 0:2, :]
        xn = ering[:, 2:4, :].rearrange("p a (t f) -> p (a t) f", f=F)
        tmp_dec = f1b[:, :, :, :].rearrange("p a h (k n) -> p a (h k) n", n=BK)
        x1s = ering[:, 0:2, :].bitcast(F16).rearrange("p a (t c) -> p (a t) c", c=2 * F)
        dtmp = f1b[:, 0, :, :].rearrange("p h (k f) -> p (h k) f", f=F)
        utmp = f1b[:, 1, :, :].rearrange("p h (k f) -> p (h k) f", f=F)
        ybuf = agg[:, 0, :].rearrange("p (k f) -> p k f", f=F)

        s = {k: sem(k) for k in (
            "zeroed", "w_in", "x_in", "mlp_in", "cols_in", "ident_set", "ones_set",
            "wv_done", "wv_copied", "xw_full", "xw_free", "f1_full", "f1_copied", "f1_stored",
            "tanh_done", "e_ready", "p_ready", "e_used", "vx_ready", "mask_conv",
            "evacuated", "stats_done", "den_stored", "den_in", "rec_made", "rec_stored", "rden_in", "agg_done",
            "bn_mv", "bn_sd", "bn_step", "xn_ready", "z_full", "e_made", "z_free",
            "elu_step", "emb_ready", "tr_full", "tr_copied", "yc_full", "yc_exp", "yc_done",
            "xn_in", "ln_step", "ln_sd", "x1_done", "hi_made", "d_made", "lo_made",
            "u_full", "u_free", "lo_scaled", "deg_step", "deg_sqrt", "y_step", "y_sqrt", "y_ready",
            "fin_step", "held")}
        f1_in = [sem(f"f1_in{b}") for b in range(2)]
        mask_in = [sem(f"mask_in{k}") for k in range(RING)]
        stage_in = [sem(f"stage_in{k}") for k in range(2)]
        adj_stored = [sem(f"adj_stored{k}") for k in range(RING)]
        adjg_in = [sem(f"adjg_in{k}") for k in range(2)]
        y_free = [sem(f"y_free{k}") for k in range(GT)]

        def first_visit(p):
            return p in (0, NB)

        def visit(p):
            return sum(first_visit(q) for q in range(p))

        def reload(p):
            return p - visit(p)

        def chunk(p):
            return (p % PASSES) // NB

        def pair(p):
            return p % NB

        def tile_of(it, u):
            return it * RING + u

        def evacuations(p):
            return 4 * (p + 1) if p < PASSES else 4 * PASSES + 2 * (p + 1 - PASSES)

        def very_first(p, it):
            return p == 0 and isinstance(it, int) and it == 0

        def held(eng):
            eng.sem_inc(s["held"], 1)

        block = ctx.enter_context(nc.Block())

        @block.sync
        def _(sp):
            for b in range(NB):
                sp.dma_start(xTs[:, b, :], xT[b * P:(b + 1) * P, :]).then_inc(s["x_in"], 16)
            sp.wait_ge(s["zeroed"], 3)
            with nc.allow_non_contiguous_dma(reason="single columns of the small V"):
                for h in range(H):
                    rows, b, c = slice(D * (h % 2), D * (h % 2) + D), h // 2, D * (h % 2)
                    sp.dma_start(wm[rows, b, c:c + D], W[h]).then_inc(s["w_in"], 16)
                    sp.dma_start(wtbd[rows, b, c:c + D], WT[h]).then_inc(s["w_in"], 16)
                    sp.dma_start(vbd[rows, b, h:h + 1], V[h, 0]).then_inc(s["w_in"], 16)
                    sp.dma_start(vbd[rows, b, H + h:H + h + 1], V[h, 1]).then_inc(s["w_in"], 16)
                for k, v in enumerate((enc_g, enc_b, encm_bias, encm_g, encm_b, decm_bias, decm_g, decm_b)):
                    sp.dma_start(cols[:, :, k], v.rearrange("(b p) -> p b", p=P)).then_inc(s["cols_in"], 16)
            sp.dma_start(wenc[:, :, :], encm_WT.rearrange("(b p) o -> p b o", p=P)).then_inc(s["mlp_in"], 16)
            sp.dma_start(wdec[:, :, :], decm_WT.rearrange("(b p) o -> p b o", p=P)).then_inc(s["mlp_in"], 16)
            sp.wait_ge(s["f1_copied"], NC)
            sp.dma_start(f1_d, f1row).then_inc(s["f1_stored"], 16)
            sp.wait_ge(s["f1_stored"], 16)

            def load_f1(p):
                for h in range(HP):
                    src = f1_d[pair(p) * HP + h:pair(p) * HP + h + 1, chunk(p) * CH:(chunk(p) + 1) * CH]
                    sp.dma_start(f1b[:, p % 2, h, :], src.to_broadcast([P, CH])).then_inc(f1_in[p % 2], 16)

            load_f1(0)
            load_f1(1)

            def bring_adj(p, it):
                for u in range(RING):
                    n = tile_of(it, u)
                    k = visit(p) * NT + n
                    if not (very_first(p, it) and u < 2):
                        sp.wait_ge(s["mask_conv"], k - 1)
                    sp.dma_start(stage[:, u % 2, :], adjT[ds(n * P, P), chunk(p) * CH:(chunk(p) + 1) * CH])\
                        .then_inc(stage_in[u % 2], 16)
                    if u > 0:
                        store_adj8(p, n - 1, u - 1)
                store_adj8(p, tile_of(it, RING - 1), RING - 1)

            def store_adj8(p, n, slot):
                sp.wait_ge(s["mask_conv"], visit(p) * NT + n + 1)
                sp.dma_start(adj8[ds(n * P, P), chunk(p) * CH // 4:(chunk(p) + 1) * CH // 4], mask_w[:, slot, :])\
                    .then_inc(adj_stored[slot], 16)

            def load_masks(p, it):
                for u in range(RING):
                    n = tile_of(it, u)
                    sp.wait_ge(s["p_ready"], NT * p + n - RING + 1)
                    sp.dma_start(mask_w[:, u, :], adj8[ds(n * P, P), chunk(p) * CH // 4:(chunk(p) + 1) * CH // 4])\
                        .then_inc(mask_in[u], 16)

            def spread_den(p):
                sp.wait_ge(s["evacuated"], evacuations(p))
                for h in range(HP):
                    sp.dma_start(den_d[pair(p) * HP + h:pair(p) * HP + h + 1, chunk(p) * CH:(chunk(p) + 1) * CH],
                                 rden[D * h:D * h + 1, :]).then_inc(s["den_stored"], 16)
                sp.wait_ge(s["den_stored"], 32 * (p + 1))
                for h in range(HP):
                    src = den_d[pair(p) * HP + h, chunk(p) * CH:(chunk(p) + 1) * CH]
                    sp.dma_start(dsm[D * h:D * h + D, :], src.rearrange("(q c) -> q c", c=32))\
                        .then_inc(s["den_in"], 16)

            def spread_rec(p):
                sp.wait_ge(s["rec_made"], 2 * (p + 1))
                for h in range(HP):
                    dst = rec_d[pair(p) * HP + h, chunk(p) * CH:(chunk(p) + 1) * CH]
                    sp.dma_start(dst.rearrange("(q c) -> q c", c=32), rsm[D * h:D * h + D, :])\
                        .then_inc(s["rec_stored"], 16)
                sp.wait_ge(s["rec_stored"], 32 * (p + 1))
                load_rec(p)

            def load_rec(p):
                for h in range(HP):
                    src = rec_d[pair(p) * HP + h:pair(p) * HP + h + 1, chunk(p) * CH:(chunk(p) + 1) * CH]
                    sp.dma_start(rden[D * h:D * h + D, :], src.to_broadcast([D, CH])).then_inc(s["rden_in"], 16)

            for p in range(2 * PASSES):
                tiles = bring_adj if first_visit(p) else load_masks
                if p == 1:
                    for k in range(RING):
                        sp.wait_ge(adj_stored[k], 16 * ITS)
                if p == NB + 1:
                    for k in range(RING):
                        sp.wait_ge(adj_stored[k], 32 * ITS)
                tiles(p, 0)
                if 1 <= p < PASSES:
                    spread_den(p - 1)
                if p > PASSES:
                    sp.wait_ge(s["agg_done"], p - 1)
                    load_rec(p - 1)
                tiles(p, 1)
                if 1 <= p < PASSES:
                    spread_rec(p - 1)
                if 1 <= p and p + 1 < 2 * PASSES:
                    sp.wait_ge(s["tanh_done"], NT * p)
                    load_f1(p + 1)
                with sp.Fori(2, ITS) as it:
                    tiles(p, it)
                if p == PASSES - 1:
                    spread_den(p)
                    spread_rec(p)
            sp.wait_ge(s["agg_done"], 2 * PASSES - 1)
            load_rec(2 * PASSES - 1)

            sp.wait_ge(s["e_used"], 2 * PASSES * NT)
            sp.dma_start(xn, x.rearrange("(t p) f -> p t f", p=P)).then_inc(s["xn_in"], 16)

            sp.wait_ge(s["agg_done"], 2 * PASSES)
            adj_v = adj8.rearrange("(t p) n -> p t n", p=P)

            def load_group(g, slot):
                sp.dma_start(adjg_w[:, slot, :, :], adj_v[:, :, ds(g * (GI // 4), GI // 4)]).then_inc(adjg_in[slot], 16)

            def store_group(g):
                for k in range(GT):
                    sp.wait_ge(s["y_ready"], GT * g + k + 1)
                    sp.dma_start(out[ds(g * GI + k * P, P), :], ybuf[:, k, :]).then_inc(y_free[k], 16)

            load_group(0, 0)
            load_group(1, 1)
            with sp.Fori(0, NG // 2 - 1) as gg:
                for v in range(2):
                    sp.wait_ge(s["u_full"], GT * (2 * gg + v + 1))
                    load_group(2 * gg + v + 2, v)
                    store_group(2 * gg + v)
            for g in range(NG - 2, NG):
                store_group(g)
            for k in range(GT):
                sp.wait_ge(y_free[k], 16 * NG + 16)

        @block.gpsimd
        def _(pool):
            pool.memset(wm[:, :, :], 0.0).then_inc(s["zeroed"], 1)
            pool.memset(wtbd[:, :, :], 0.0).then_inc(s["zeroed"], 1)
            pool.memset(vbd[:, :, :], 0.0).then_inc(s["zeroed"], 1)
            pool.memset(ident[:, :], 0.0).then_inc(s["ident_set"], 1)
            pool.wait_ge(s["ident_set"], 1)
            pool.affine_select(out=ident[:, :], in_=ident[:, :], compare_op=ALU.not_equal, fill=1.0,
                               base=0, pattern=[[-1, P]], channel_multiplier=1).then_inc(s["ident_set"], 1)
            pool.memset(vx[:, :, :, :], 1.0).then_inc(s["ones_set"], 1)
            pool.memset(ones16[:, :], 1.0).then_inc(s["ones_set"], 1)
            pool.memset(eps[:, 0:1], EPS_BN).then_inc(s["ones_set"], 1)
            pool.memset(eps[:, 1:2], EPS_LN).then_inc(s["ones_set"], 1)
            pool.wait_ge(s["ones_set"], 4)

            def steps(p, it):
                for u in range(RING):
                    n = tile_of(it, u)
                    m = NT * p + n
                    if first_visit(p):
                        k = visit(p) * NT + n
                        pool.wait_ge(stage_in[u % 2], 16 * (visit(p) * NT // 2 + it * 2 + u // 2 + 1))
                        if not very_first(p, it):
                            pool.wait_ge(s["p_ready"], m - RING + 1)
                            pool.wait_ge(adj_stored[u], 16 * (visit(p) * ITS + it))
                        held(pool)
                        pool.tensor_copy(mask[:, u, :], stage[:, u % 2, :], saturate=False)\
                            .then_inc(s["mask_conv"], 1)
                    if not very_first(p, it):
                        pool.wait_ge(s["e_used"], m - RING + 1)
                    pool.tensor_copy(vx[:, u, :, 0:D],
                                     vals[:, ds(n, 1), pair(p) * P:(pair(p) + 1) * P]
                                     .rearrange("p a (h d) -> p (a h) d", h=HP)).then_inc(s["vx_ready"], 1)

            for p in range(2 * PASSES):
                if p == 0:
                    pool.wait_ge(s["xw_free"], NT)
                if p == PASSES:
                    pool.wait_ge(s["tr_copied"], NT)
                steps(p, 0)
                with pool.Fori(1, ITS) as it:
                    steps(p, it)

        @block.scalar
        def _(act):
            def tanh(p, it, u):
                n = tile_of(it, u)
                m = NT * p + n
                if not very_first(p, it):
                    act.wait_ge(s["e_used"], m - RING + 1)
                for h in range(HP):
                    k = pair(p) * HP + h
                    last = act.activation(ering[:, u, h * CH:(h + 1) * CH], f1b[:, p % 2, h, :], ACT.Tanh,
                                          bias=f2h[:, ds(n, 1), k],
                                          scale=0.5)
                last.then_inc(s["tanh_done"], 1)

            def exp(p, n, slot):
                act.wait_ge(s["tanh_done"], NT * p + n + 1)
                act.activation(ering[:, slot, :], ering[:, slot, :], ACT.Exp, scale=0.5)\
                    .then_inc(s["e_ready"], 1)

            def steps(p, it):
                for u in range(RING):
                    tanh(p, it, u)
                    if not (very_first(p % PASSES, it) and u == 0):
                        exp(p, tile_of(it, u) - 1, (u - 1) % RING)

            def elu_exp(tmp, bias, base, full, done):
                with act.Fori(0, NC // 2) as i:
                    for v in range(4):
                        act.wait_ge(s[full], base + 4 * i + v + 1)
                        act.activation(tmp[:, 0, v, :], ps[:, v, :], ACT.Exp,
                                       bias=cols[:, v % 2, bias:bias + 1] if bias is not None else 0.0)\
                            .then_inc(s[done], 1)

            def bn_sqrt(k):
                act.wait_ge(s["bn_mv"], k + 1)
                act.activation(bnc[:, :, 0], mv[:, :, 1], ACT.Sqrt, bias=eps[:, 0:1]).then_inc(s["bn_sd"], 1)

            def copy_transposed(base):
                with act.Fori(0, ITS) as it:
                    for u in range(RING):
                        act.wait_ge(s["tr_full"], base + it * RING + u + 1)
                        act.activation(vals[:, ds(it * RING + u, 1), :], ps[:, u:u + 1, 0:F], ACT.Copy)\
                            .then_inc(s["tr_copied"], 1)

            act.wait_ge(s["xw_free"], NT)
            for p in range(2 * PASSES):
                if p == PASSES:
                    exp(p - 1, NT - 1, RING - 1)
                    act.wait_ge(s["cols_in"], 16 * 8)
                    act.wait_ge(s["ones_set"], 4)
                    bn_sqrt(0)
                    elu_exp(tmp_enc, 2, 0, "z_full", "e_made")
                    bn_sqrt(1)
                    copy_transposed(0)
                act.wait_ge(f1_in[p % 2], 32 * (p // 2 + 1))
                steps(p, 0)
                with act.Fori(1, ITS) as it:
                    steps(p, it)
            exp(2 * PASSES - 1, NT - 1, RING - 1)

            elu_exp(tmp_dec, None, 0, "yc_full", "yc_exp")
            elu_exp(tmp_dec, 5, 2 * NC, "z_full", "e_made")
            bn_sqrt(2)
            act.wait_ge(s["ln_step"], 2 * NT)
            act.activation(lnsd[:, :, 0], lnmv[:, :, 1], ACT.Sqrt, bias=eps[:, 1:2]).then_inc(s["ln_sd"], 1)
            for k in range(4):
                t = slice(8 * k, 8 * k + 8)
                act.wait_ge(s["x1_done"], 8 * k + 8)
                act.activation(x1s[:, t, 0:F], vals[:, t, :], ACT.Copy).then_inc(s["hi_made"], 1)
                if k > 0:
                    act.wait_ge(s["d_made"], k)
                    act.activation(x1s[:, 8 * k - 8:8 * k, F:2 * F], dtmp[:, 8 * (k - 1) % 16:8 * (k - 1) % 16 + 8, :],
                                   ACT.Copy, scale=LO_SCALE).then_inc(s["lo_made"], 1)
            act.wait_ge(s["d_made"], 4)
            act.activation(x1s[:, 24:32, F:2 * F], dtmp[:, 8:16, :], ACT.Copy, scale=LO_SCALE)\
                .then_inc(s["lo_made"], 1)

            with act.Fori(0, NG) as g:
                for k in range(GT):
                    act.wait_ge(s["u_full"], GT * g + k + 1)
                    act.activation(utmp[:, k, :], ps[:, k, F:2 * F], ACT.Copy, scale=1.0 / LO_SCALE)\
                        .then_inc(s["lo_scaled"], 1)
                    act.activation(degs[:, k, 0:1], ps[:, 4 + k, 0:1], ACT.Sqrt).then_inc(s["deg_sqrt"], 1)
                    act.wait_ge(s["y_step"], 3 * (GT * g + k) + 3)
                    act.activation(degs[:, k, 7:8], lnmv[:, k, 1:2], ACT.Sqrt, bias=eps[:, 1:2])\
                        .then_inc(s["y_sqrt"], 1)

        @block.vector
        def _(dve):
            dve.wait_ge(s["wv_done"], 1)
            dve.tensor_copy(wm[:, :, P:P + 2 * H],
                            ps[:, 0, 0:NB * 2 * H].rearrange("p (b c) -> p b c", b=NB)).then_inc(s["wv_copied"], 1)
            with dve.Fori(0, NC // 4) as i:
                for u in range(4):
                    dve.wait_ge(s["f1_full"], 4 * i + u + 1)
                    dve.tensor_copy(agg[0:H, 0, ds((4 * i + u) * BK, BK)], ps[0:H, u, :])\
                        .then_inc(s["f1_copied"], 1)
            with dve.Fori(0, ITS) as it:
                for u in range(RING):
                    n = tile_of(it, u)
                    bank = ps[:, 4 + u, 0:NB * (P + 2 * H)].rearrange("p (b c) -> p b c", b=NB)
                    dve.wait_ge(s["xw_full"], n + 1)
                    dve.tensor_copy(vals[:, ds(n, 1), :].rearrange("p a (b c) -> p (a b) c", b=NB), bank[:, :, 0:P])
                    for b in range(NB):
                        last = dve.tensor_scalar(f2h[:, ds(n, 1), b * HP:(b + 1) * HP],
                                                 bank[:, b:b + 1, P + H + b * HP:P + H + (b + 1) * HP],
                                                 0.5, None, ALU.mult)
                    last.then_inc(s["xw_free"], 1)

            def masks(p, it):
                for u in range(RING):
                    n = tile_of(it, u)
                    dve.wait_ge(s["e_ready"], NT * p + n + 1)
                    if first_visit(p):
                        dve.wait_ge(s["mask_conv"], visit(p) * NT + n + 1)
                    else:
                        dve.wait_ge(mask_in[u], 16 * (reload(p) * ITS + it + 1))
                    held(dve)
                    e = ering[:, u, :].rearrange("p (h n) -> p h n", h=HP)
                    dve.tensor_tensor(e, e, mask[:, u:u + 1, :].to_broadcast([P, HP, CH]), ALU.mult)\
                        .then_inc(s["p_ready"], 1)

            def evacuate(p):
                dve.wait_ge(s["e_used"], NT * (p + 1))
                for h in range(HP):
                    rows = slice(D * h, D * h + D)
                    src = ps[0:D, 4 * h:4 * h + 4, :]
                    dve.tensor_copy(agg[rows, pair(p), chunk(p) * CH:(chunk(p) + 1) * CH]
                                    .rearrange("p (k n) -> p k n", k=4), src).then_inc(s["evacuated"], 1)
                    if p < PASSES:
                        dve.tensor_copy(rden[D * h:D * h + 1, :].rearrange("p (k n) -> p k n", k=4),
                                        ps[D:D + 1, 4 * h:4 * h + 4, :]).then_inc(s["evacuated"], 1)

            def reciprocals(p):
                dve.wait_ge(s["den_in"], 32 * (p + 1))
                dve.tensor_scalar(dsm[:, :], dsm[:, :], TINY, None, ALU.max).then_inc(s["rec_made"], 1)
                dve.wait_ge(s["rec_made"], 2 * p + 1)
                dve.reciprocal(rsm[:, :], dsm[:, :]).then_inc(s["rec_made"], 1)

            def normalise(p):
                dve.wait_ge(s["rden_in"], 32 * (p + 1))
                dve.wait_ge(s["evacuated"], evacuations(p))
                a = agg[:, pair(p), chunk(p) * CH:(chunk(p) + 1) * CH]
                dve.tensor_tensor(a, a, rden[:, :], ALU.mult).then_inc(s["agg_done"], 1)
                if p < PASSES:
                    dve.wait_ge(s["agg_done"], p + 1)
                    for k in range(4):
                        c = chunk(p) * 4 + k
                        last = dve.bn_stats(stats[:, pair(p), c, :], agg[:, pair(p), c * BK:(c + 1) * BK])
                    return last

            step = [0]

            def link(ins):
                step[0] += 1
                ins.then_inc(s["bn_step"], 1)
                dve.wait_ge(s["bn_step"], step[0])

            def bn_coefficients(k, gamma, beta):
                for b in range(NB):
                    last = dve.bn_aggr(mv[:, b, :], stats[:, b, :, :].rearrange("p c s -> p (c s)"))
                last.then_inc(s["bn_mv"], 1)
                dve.wait_ge(s["bn_mv"], k + 1)
                dve.wait_ge(s["bn_sd"], k + 1)
                link(dve.reciprocal(bnc[:, :, 1], bnc[:, :, 0]))
                link(dve.tensor_tensor(bnc[:, :, 1], bnc[:, :, 1], cols[:, :, gamma], ALU.mult))
                link(dve.tensor_tensor(bnc[:, :, 2], mv[:, :, 0], bnc[:, :, 1], ALU.mult))
                link(dve.tensor_tensor(bnc[:, :, 3], cols[:, :, beta], bnc[:, :, 2], ALU.subtract))

            def affine(buf, b, c, n, name):
                v = buf[:, b, c:c + n]
                dve.tensor_scalar(v, v, bnc[:, b, 1:2], bnc[:, b, 3:4], ALU.mult, ALU.add).then_inc(s[name], 1)

            def elu_plus(src, tmp, dst, bias, base, steps_before):
                with dve.Fori(0, NC // 2) as i:
                    for v in range(4):
                        o, c = v % 2, 2 * i + v // 2
                        cc = ds(c * BK, BK)
                        at = steps_before + (4 * i + v) * 3
                        e, u = tmp[:, 0, v, :], tmp[:, 1, v, :]
                        dve.wait_ge(s["e_made"], base + 4 * i + v + 1)
                        dve.tensor_scalar(e, e, 1.0, -1.0, ALU.min, ALU.add).then_inc(s["elu_step"], 1)
                        dve.wait_ge(s["elu_step"], at + 1)
                        dve.scalar_tensor_tensor(out=u, in0=ps[:, v, :], scalar=cols[:, o, bias:bias + 1],
                                                 in1=e, op0=ALU.add, op1=ALU.max).then_inc(s["elu_step"], 1)
                        dve.wait_ge(s["elu_step"], at + 2)
                        dve.tensor_tensor(dst[:, o, cc], u, src[:, o, cc], ALU.add).then_inc(s["elu_step"], 1)
                        dve.wait_ge(s["elu_step"], at + 3)
                        dve.bn_stats(stats[:, o, ds(c, 1), :], dst[:, o, cc]).then_inc(s["z_free"], 1)

            def elu(tmp, dst, steps_before):
                with dve.Fori(0, NC // 2) as i:
                    for v in range(4):
                        e = tmp[:, 0, v, :]
                        dve.wait_ge(s["yc_exp"], 4 * i + v + 1)
                        dve.tensor_scalar(e, e, 1.0, -1.0, ALU.min, ALU.add).then_inc(s["elu_step"], 1)
                        dve.wait_ge(s["elu_step"], steps_before + 4 * i + v + 1)
                        dve.tensor_tensor(dst[:, v % 2, ds((2 * i + v // 2) * BK, BK)], ps[:, v, :], e, ALU.max)\
                            .then_inc(s["yc_done"], 1)

            for p in range(2 * PASSES):
                if p == PASSES:
                    evacuate(p - 1)
                    reciprocals(p - 1)
                    normalise(p - 1).then_inc(s["stats_done"], 1)
                    dve.wait_ge(s["stats_done"], 1)
                    dve.wait_ge(s["cols_in"], 16 * 8)
                    bn_coefficients(0, 0, 1)
                    for c in range(NC):
                        for b in range(NB):
                            affine(agg, b, c * BK, BK, "xn_ready")
                    dve.wait_ge(s["xn_ready"], 2 * NC)
                    elu_plus(agg, tmp_enc, h_enc, 2, 0, 0)
                    dve.wait_ge(s["z_free"], 2 * NC)
                    bn_coefficients(1, 3, 4)
                    for c in range(NC):
                        for b in range(NB):
                            affine(h_enc, b, c * BK, BK, "emb_ready")
                elif p:
                    evacuate(p - 1)
                masks(p, 0)
                if 1 <= p < PASSES:
                    reciprocals(p - 1)
                masks(p, 1)
                masks(p, 2)
                if 1 <= p and p != PASSES:
                    normalise(p - 1)
                with dve.Fori(3, ITS) as it:
                    masks(p, it)
            evacuate(2 * PASSES - 1)
            normalise(2 * PASSES - 1)

            elu(tmp_dec, yc, 6 * NC)
            dve.wait_ge(s["yc_done"], 2 * NC)
            elu_plus(yc, tmp_dec, agg, 5, 2 * NC, 8 * NC)
            dve.wait_ge(s["z_free"], 4 * NC)
            bn_coefficients(2, 6, 7)
            for c in range(NC):
                for b in range(NB):
                    affine(agg, b, c * BK, BK, "emb_ready")
            dve.wait_ge(s["xn_in"], 16)
            with dve.Fori(0, ITS) as it:
                for u in range(RING):
                    n = tile_of(it, u)
                    dve.wait_ge(s["tr_full"], NT + n + 1)
                    dve.tensor_tensor(vals[:, ds(n, 1), :], ps[:, u:u + 1, 0:F], xn[:, ds(n, 1), :], ALU.add)\
                        .then_inc(s["tr_copied"], 1)
                    dve.wait_ge(s["tr_copied"], NT + n + 1)
                    dve.bn_stats(lnst[:, ds(n, 1), :], vals[:, ds(n, 1), :]).then_inc(s["ln_step"], 1)
            dve.wait_ge(s["ln_step"], NT)
            for n in range(NT):
                dve.bn_aggr(lnmv[:, n, :], lnst[:, n, :]).then_inc(s["ln_step"], 1)
            dve.wait_ge(s["ln_sd"], 1)
            dve.reciprocal(lnsd[:, :, 1], lnsd[:, :, 0]).then_inc(s["ln_step"], 1)
            dve.wait_ge(s["ln_step"], 2 * NT + 1)
            for n in range(NT):
                dve.tensor_scalar(vals[:, n, :], vals[:, n, :], lnmv[:, n, 0:1], lnsd[:, n, 1:2],
                                  ALU.subtract, ALU.mult).then_inc(s["x1_done"], 1)
            for k in range(4):
                t = slice(8 * k, 8 * k + 8)
                dve.wait_ge(s["hi_made"], k + 1)
                if k >= 2:
                    dve.wait_ge(s["lo_made"], k - 1)
                dve.tensor_tensor(dtmp[:, 8 * k % 16:8 * k % 16 + 8, :], vals[:, t, :], x1s[:, t, 0:F],
                                  ALU.subtract).then_inc(s["d_made"], 1)

            for k in range(GT):
                dve.memset(ybuf[:, k, 0:1], 0.0).then_inc(y_free[k], 16)
            dve.memset(degs[:, :, :], 0.0).then_inc(s["u_free"], GT)
            with dve.Fori(0, NG) as g:
                for k in range(GT):
                    r = GT * g + k
                    d = degs[:, k, :]
                    dve.wait_ge(s["lo_scaled"], r + 1)
                    dve.tensor_tensor(utmp[:, k, :], ps[:, k, 0:F], utmp[:, k, :], ALU.add)\
                        .then_inc(s["deg_step"], 1)
                    dve.wait_ge(s["deg_sqrt"], r + 1)
                    dve.tensor_copy(d[:, 1:2], ps[:, 4 + k, 0:1]).then_inc(s["u_free"], 1)
                    dve.tensor_scalar(d[:, 2:3], d[:, 0:1], EPS_NORM, None, ALU.max).then_inc(s["deg_step"], 1)
                    dve.wait_ge(s["deg_step"], 7 * r + 2)
                    dve.reciprocal(d[:, 3:4], d[:, 2:3]).then_inc(s["deg_step"], 1)
                    dve.wait_ge(s["deg_step"], 7 * r + 3)
                    dve.tensor_scalar(d[:, 4:5], d[:, 3:4], 1.0, None, ALU.add).then_inc(s["deg_step"], 1)
                    dve.wait_ge(s["deg_step"], 7 * r + 4)
                    dve.wait_ge(s["u_free"], GT + r + 1)
                    dve.tensor_tensor(d[:, 5:6], d[:, 4:5], d[:, 1:2], ALU.mult).then_inc(s["deg_step"], 1)
                    dve.wait_ge(s["deg_step"], 7 * r + 5)
                    dve.reciprocal(d[:, 6:7], d[:, 5:6]).then_inc(s["deg_step"], 1)
                    dve.wait_ge(s["deg_step"], 7 * r + 6)
                    dve.tensor_tensor(d[:, 6:7], d[:, 6:7], d[:, 4:5], ALU.mult).then_inc(s["deg_step"], 1)
                    dve.wait_ge(s["deg_step"], 7 * r + 7)
                    dve.scalar_tensor_tensor(out=utmp[:, k, :], in0=utmp[:, k, :], scalar=d[:, 6:7],
                                             in1=vals[:, ds(r, 1), :].rearrange("p a f -> p (a f)"),
                                             op0=ALU.mult, op1=ALU.add).then_inc(s["y_step"], 1)
                    dve.wait_ge(s["y_step"], 3 * r + 1)
                    dve.bn_stats(lnst[:, k, :], utmp[:, k, :]).then_inc(s["y_step"], 1)
                    dve.wait_ge(s["y_step"], 3 * r + 2)
                    held(dve)
                    dve.bn_aggr(lnmv[:, k, :], lnst[:, k, :]).then_inc(s["y_step"], 1)
                    dve.wait_ge(s["y_sqrt"], r + 1)
                    dve.reciprocal(lnsd[:, k, 1:2], degs[:, k, 7:8]).then_inc(s["fin_step"], 1)
                    dve.wait_ge(s["fin_step"], r + 1)
                    dve.wait_ge(y_free[k], 16 * g + 16)
                    dve.tensor_scalar(ybuf[:, k, :], utmp[:, k, :], lnmv[:, k, 0:1], lnsd[:, k, 1:2],
                                      ALU.subtract, ALU.mult).then_inc(s["y_ready"], 1)

        @block.tensor
        def _(pe):
            pe.wait_ge(s["w_in"], 16 * 4 * H)
            for b in range(NB):
                last = pe.matmul(ps[:, 0, b * 2 * H:(b + 1) * 2 * H], wtbd[:, b, :], vbd[:, b, :],
                                 start=True, stop=True)
            last.then_inc(s["wv_done"], 1)
            pe.wait_ge(s["wv_copied"], 1)
            pe.wait_ge(s["x_in"], 16 * NB)
            for c in range(NC):
                if c >= 4:
                    pe.wait_ge(s["f1_copied"], c - 3)
                for b in range(NB):
                    last = pe.matmul(ps[0:H, c % 4, :], wm[:, b, P:P + H], xTs[:, b, c * BK:(c + 1) * BK],
                                     start=(b == 0), stop=(b == NB - 1))
                last.then_inc(s["f1_full"], 1)
            for n in range(NT):
                if n >= RING:
                    pe.wait_ge(s["xw_free"], n - RING + 1)
                for b in range(NB):
                    last = pe.matmul(ps[:, 4 + n % RING, b * (P + 2 * H):(b + 1) * (P + 2 * H)],
                                     xTs[:, b, n * P:(n + 1) * P], wm[:, b, :], start=True, stop=True)
                last.then_inc(s["xw_full"], 1)
            pe.wait_ge(s["xw_free"], NT)
            pe.wait_ge(s["f1_copied"], NC)

            def steps(p, it):
                for u in range(RING):
                    n = tile_of(it, u)
                    m = NT * p + n
                    fixed = isinstance(it, int)
                    start, stop = fixed and it == 0 and u == 0, fixed and it == ITS - 1 and u == RING - 1
                    pe.wait_ge(s["vx_ready"], m + 1)
                    pe.wait_ge(s["p_ready"], m + 1)
                    for h in range(HP):
                        if start and p % PASSES:
                            before = evacuations(p - 1) - evacuations(p - 2) if p > 1 else 4
                            pe.wait_ge(s["evacuated"], evacuations(p - 1) - (HP - 1 - h) * before // HP)
                        for c in range(4):
                            last = pe.matmul(ps[0:D + 1, 4 * h + c, :], vx[:, u, h, :],
                                             ering[:, u, h * CH + c * BK:h * CH + (c + 1) * BK],
                                             start=start, stop=stop)
                    last.then_inc(s["e_used"], 1)

            def mlp(w, src, base, ready, free):
                for c in range(NC):
                    if ready:
                        pe.wait_ge(s[ready], 2 * c + 2)
                    for o in range(NB):
                        k = 2 * c + o
                        if k >= 4:
                            pe.wait_ge(s[free], base + k - 3)
                        for b in range(NB):
                            last = pe.matmul(ps[:, k % 4, :], w[:, b, o * P:(o + 1) * P],
                                             src[:, b, c * BK:(c + 1) * BK], start=(b == 0), stop=(b == NB - 1))
                        last.then_inc(s["z_full"], 1)

            def transposes(src, base):
                for n in range(NT):
                    if n % 4 == 0:
                        pe.wait_ge(s["emb_ready"], 2 * base // NT * NC + 2 * (n // 4) + 2)
                    if n >= RING:
                        pe.wait_ge(s["tr_copied"], base + n - RING + 1)
                    for b in range(NB):
                        last = pe.transpose(ps[:, n % RING, b * P:(b + 1) * P], src[:, b, n * P:(n + 1) * P],
                                            ident[:, :])
                    last.then_inc(s["tr_full"], 1)

            for p in range(2 * PASSES):
                if p == PASSES:
                    pe.wait_ge(s["mlp_in"], 32)
                    pe.wait_ge(s["evacuated"], 4 * PASSES)
                    mlp(wenc, agg, 0, "xn_ready", "z_free")
                    pe.wait_ge(s["z_free"], 2 * NC)
                    pe.wait_ge(s["ident_set"], 2)
                    transposes(h_enc, 0)
                    pe.wait_ge(s["tr_copied"], NT)
                steps(p, 0)
                with pe.Fori(1, ITS - 1) as it:
                    steps(p, it)
                steps(p, ITS - 1)

            for c in range(NC):
                if c == 0:
                    pe.wait_ge(s["agg_done"], 2 * PASSES)
                for o in range(NB):
                    k = 2 * c + o
                    if k >= 4:
                        pe.wait_ge(s["yc_done"], k - 3)
                    pe.matmul(ps[:, k % 4, :], wtbd[:, o, :], agg[:, o, c * BK:(c + 1) * BK],
                              start=True, stop=True).then_inc(s["yc_full"], 1)
            pe.wait_ge(s["yc_done"], 2 * NC)
            mlp(wdec, yc, 2 * NC, None, "z_free")
            pe.wait_ge(s["z_free"], 4 * NC)
            transposes(agg, NT)
            pe.wait_ge(s["tr_copied"], 2 * NT)

            pe.wait_ge(s["lo_made"], 4)
            with pe.Fori(0, NG // 2) as gg:
                for v in range(2):
                    g = 2 * gg + v
                    pe.wait_ge(adjg_in[v], 16 * (gg + 1))
                    for k in range(GT):
                        pe.wait_ge(s["u_free"], GT * g + k + 1)
                        held(pe)
                        for t in range(NT):
                            w = adjg[:, v, t, k * P:(k + 1) * P]
                            pe.matmul(ps[:, 4 + k, 0:2], w, ones16[:, :], start=(t == 0), stop=(t == NT - 1))
                            last = pe.matmul(ps[:, k, :], w, x1s[:, t, :], start=(t == 0), stop=(t == NT - 1))
                        last.then_inc(s["u_full"], 1)


def kernel(x, adj, L0_gnn_W, L0_gnn_V, L0_gnn_enc_bn_gamma, L0_gnn_enc_bn_beta, L0_gnn_enc_mlp_W,
           L0_gnn_enc_mlp_b, L0_gnn_enc_mlp_bn_gamma, L0_gnn_enc_mlp_bn_beta, L0_gnn_dec_mlp_W,
           L0_gnn_dec_mlp_b, L0_gnn_dec_mlp_bn_gamma, L0_gnn_dec_mlp_bn_beta):
    import numpy as np
    import concourse.bacc as bacc
    from concourse.bass_utils import run_bass_kernel_spmd

    x, adj, W = np.asarray(x), np.asarray(adj), np.asarray(L0_gnn_W)
    host = {
        "xT": x.T, "x": x, "adjT": adj.T, "W": W, "WT": W.transpose(0, 2, 1), "V": L0_gnn_V,
        "enc_g": L0_gnn_enc_bn_gamma, "enc_b": L0_gnn_enc_bn_beta,
        "encm_WT": np.asarray(L0_gnn_enc_mlp_W).T, "encm_bias": L0_gnn_enc_mlp_b,
        "encm_g": L0_gnn_enc_mlp_bn_gamma, "encm_b": L0_gnn_enc_mlp_bn_beta,
        "decm_WT": np.asarray(L0_gnn_dec_mlp_W).T, "decm_bias": L0_gnn_dec_mlp_b,
        "decm_g": L0_gnn_dec_mlp_bn_gamma, "decm_b": L0_gnn_dec_mlp_bn_beta,
    }
    nc = bacc.Bacc("TRN2", target_bir_lowering=False, num_devices=1)
    arrays, args = {}, []
    for name, a in host.items():
        a = np.ascontiguousarray(a)
        arrays[f"in_{name}"] = a
        args.append(nc.dram_tensor(f"in_{name}", a.shape, mybir.dt.from_np(a.dtype), kind="ExternalInput").ap())
    out = nc.dram_tensor("out", [N, F], F32, kind="ExternalOutput").ap()
    build(nc, *args, out)
    r = run_bass_kernel_spmd(nc, [arrays], core_ids=[0])
    return r.results[0]["out"]
```

```python
from contextlib import ExitStack

import concourse.bass as bass
from concourse import mybir

ALU = mybir.AluOpType
ACT = mybir.ActivationFunctionType
F32 = mybir.dt.float32
F16 = mybir.dt.float16
F8 = mybir.dt.float8e4
ds = bass.ds

P = 128
N = 4096
F = 256
H = 4
D = F // H
NT = N // P
NB = F // P
HP = 2
CH = 2048
NCH = N // CH
BK = 512
NC = N // BK
PASSES = NCH * NB
RING = 4
ITS = NT // RING
EPS_BN = 1e-6
EPS_LN = 1e-5
EPS_NORM = 1e-12
TINY = 1e-30
LO_SCALE = 2048.0
GI = 512
NG = N // GI
GT = GI // P


def build(nc, xT, x, adjT, W, WT, V, enc_g, enc_b, encm_WT, encm_bias, encm_g, encm_b,
          decm_WT, decm_bias, decm_g, decm_b, out):
    adj8 = nc.dram_tensor("adj8", [N, N // 4], F32, kind="Internal").ap()
    f1_d = nc.dram_tensor("f1_d", [H, N], F32, kind="Internal").ap()
    den_d = nc.dram_tensor("den_d", [H, N], F32, kind="Internal").ap()
    rec_d = nc.dram_tensor("rec_d", [H, N], F32, kind="Internal").ap()

    with ExitStack() as ctx:
        def sb(name, shape, dt=F32):
            return ctx.enter_context(nc.sbuf_tensor(name, shape, dt))

        def sem(name):
            return ctx.enter_context(nc.semaphore(name))

        vals = sb("vals", [P, NT, F])
        agg = sb("agg", [P, NB, N])
        ering = sb("ering", [P, RING, HP * CH])
        f1b = sb("f1b", [P, 2, HP, CH])
        io = sb("io", [P, 8192])
        vx = sb("vx", [P, RING, HP, D + 1])
        wm = sb("wm", [P, NB, P + 2 * H])
        wtbd = sb("wtbd", [P, NB, P])
        vbd = sb("vbd", [P, NB, 2 * H])
        wenc = sb("wenc", [P, NB, F])
        wdec = sb("wdec", [P, NB, F])
        cols = sb("cols", [P, NB, 8])
        f2h = sb("f2h", [P, NT, H])
        dsm = sb("dsm", [P, 32])
        rsm = sb("rsm", [P, 32])
        ident = sb("ident", [P, P])
        ones16 = sb("ones16", [P, 2], F16)
        eps = sb("eps", [P, 2])
        stats = sb("stats", [P, NB, NC, 6])
        mv = sb("mv", [P, NB, 2])
        bnc = sb("bnc", [P, 3, NB, 4])
        lnst = sb("lnst", [P, NT, 6])
        lnmv = sb("lnmv", [P, NT, 2])
        lnsd = sb("lnsd", [P, NT, 2])
        degs = sb("degs", [P, GT, 8])
        ps = ctx.enter_context(nc.psum_tensor("ps", [P, 8, BK], F32))

        mask_w = io[:, 0:RING * CH // 4].rearrange("p (s n) -> p s n", s=RING)
        mask = io[:, 0:RING * CH // 4].bitcast(F8).rearrange("p (s n) -> p s n", s=RING)
        stage = io[:, 2048:6144].rearrange("p (s n) -> p s n", s=2)
        rden = io[:, 6144:8192]
        adjg_w = io[:, :].rearrange("p (s t n) -> p s t n", s=2, t=NT)
        adjg = io[:, :].bitcast(F8).rearrange("p (s t n) -> p s t n", s=2, t=NT)
        xTs = ering[:, 2:4, :]
        f1row = agg[0:H, 0, :]
        tmp_enc = io[:, 2048:6144].rearrange("p (a k n) -> p a k n", a=2, n=BK)
        tmp_dec = f1b[:, :, :, :].rearrange("p a h (k n) -> p a (h k) n", n=BK)
        yc = ering[:, 0:2, :]
        xn = ering[:, 2:4, :].rearrange("p a (t f) -> p (a t) f", f=F)
        x1s = ering[:, 0:2, :].bitcast(F16).rearrange("p a (t c) -> p (a t) c", c=2 * F)
        dtmp = f1b[:, 0, :, :].rearrange("p h (k f) -> p (h k) f", f=F)
        utmp = f1b[:, 1, :, :].rearrange("p h (k f) -> p (h k) f", f=F)
        ybuf = agg[:, 0, :].rearrange("p (k f) -> p k f", f=F)

        s = {k: sem(k) for k in (
            "zeroed", "w_in", "mlp_in", "cols_in", "ident_set", "ones_set",
            "wv_done", "wv_copied", "xw_full", "xw_free", "f1_full", "f1_copied", "f1_stored",
            "tanh_done", "e_ready", "p_ready", "e_used", "vx_ready", "mask_conv",
            "evacuated", "den_stored", "den_in", "rec_made", "rec_stored", "rden_in", "agg_done",
            "stats_done", "scaled", "bn_mv", "bn_sd", "bn_step", "xn_ready", "z_full", "z_free", "elu_step", "y_step0",
            "h_ready", "y_full", "y_free", "yc_ready", "tr_full", "tr_copied", "emb_ready",
            "xn_in", "sum_ready", "ln_aggr", "ln_sd", "ln_rec", "x1_done", "hi_made",
            "d_made", "lo_made", "u_full", "u_free", "lo_scaled", "deg_step", "deg_sqrt", "y_step",
            "y_sqrt", "y_ready", "fin_step", "held")}
        x_in = [sem(f"x_in{k}") for k in range(4)]
        f1_in = [sem(f"f1_in{b}") for b in range(2)]
        mask_in = [sem(f"mask_in{k}") for k in range(RING)]
        stage_in = [sem(f"stage_in{k}") for k in range(2)]
        adj_stored = [sem(f"adj_stored{k}") for k in range(RING)]
        adjg_in = [sem(f"adjg_in{k}") for k in range(2)]
        out_free = [sem(f"out_free{k}") for k in range(GT)]

        def first_visit(p):
            return p in (0, NB)

        def visit(p):
            return sum(first_visit(q) for q in range(p))

        def reload(p):
            return p - visit(p)

        def chunk(p):
            return (p % PASSES) // NB

        def pair(p):
            return p % NB

        def tile_of(it, u):
            return it * RING + u

        def evacuations(p):
            return 4 * (p + 1) if p < PASSES else 4 * PASSES + 2 * (p + 1 - PASSES)

        def very_first(p, it):
            return p == 0 and isinstance(it, int) and it == 0

        def held(eng):
            eng.sem_inc(s["held"], 1)

        block = ctx.enter_context(nc.Block())

        @block.sync
        def _(sp):
            sp.wait_ge(s["zeroed"], 3)
            with nc.allow_non_contiguous_dma(reason="single columns of the small V"):
                for h in range(H):
                    rows, b, c = slice(D * (h % 2), D * (h % 2) + D), h // 2, D * (h % 2)
                    sp.dma_start(wtbd[rows, b, c:c + D], WT[h]).then_inc(s["w_in"], 16)
                    sp.dma_start(vbd[rows, b, h:h + 1], V[h, 0]).then_inc(s["w_in"], 16)
                    sp.dma_start(vbd[rows, b, H + h:H + h + 1], V[h, 1]).then_inc(s["w_in"], 16)
                    sp.dma_start(wm[rows, b, c:c + D], W[h]).then_inc(s["w_in"], 16)
                for k in range(4):
                    c = slice(k * N // 4, (k + 1) * N // 4)
                    sp.dma_start(xTs[:, :, c], xT.rearrange("(b p) n -> p b n", p=P)[:, :, c]).then_inc(x_in[k], 16)
                for k, v in enumerate((enc_g, enc_b, encm_bias, encm_g, encm_b, decm_bias, decm_g, decm_b)):
                    sp.dma_start(cols[:, :, k], v.rearrange("(b p) -> p b", p=P)).then_inc(s["cols_in"], 16)
            sp.dma_start(wenc[:, :, :], encm_WT.rearrange("(b p) o -> p b o", p=P)).then_inc(s["mlp_in"], 16)
            sp.dma_start(wdec[:, :, :], decm_WT.rearrange("(b p) o -> p b o", p=P)).then_inc(s["mlp_in"], 16)

            def store_f1(c):
                sp.wait_ge(s["f1_copied"], (c + 1) * NC // NCH)
                sp.dma_start(f1_d[:, c * CH:(c + 1) * CH], f1row[:, c * CH:(c + 1) * CH])\
                    .then_inc(s["f1_stored"], 16)
                sp.wait_ge(s["f1_stored"], 16 * (c + 1))

            def load_f1(p):
                for h in range(HP):
                    src = f1_d[pair(p) * HP + h:pair(p) * HP + h + 1, chunk(p) * CH:(chunk(p) + 1) * CH]
                    sp.dma_start(f1b[:, p % 2, h, :], src.to_broadcast([P, CH])).then_inc(f1_in[p % 2], 16)

            store_f1(0)
            load_f1(0)
            load_f1(1)

            def bring_adj(p, it):
                for u in range(RING):
                    n = tile_of(it, u)
                    k = visit(p) * NT + n
                    if not (very_first(p, it) and u < 2):
                        sp.wait_ge(s["mask_conv"], k - 1)
                    sp.dma_start(stage[:, u % 2, :], adjT[ds(n * P, P), chunk(p) * CH:(chunk(p) + 1) * CH])\
                        .then_inc(stage_in[u % 2], 16)
                    if u > 0:
                        store_adj8(p, n - 1, u - 1)
                store_adj8(p, tile_of(it, RING - 1), RING - 1)

            def store_adj8(p, n, slot):
                sp.wait_ge(s["mask_conv"], visit(p) * NT + n + 1)
                sp.dma_start(adj8[ds(n * P, P), chunk(p) * CH // 4:(chunk(p) + 1) * CH // 4], mask_w[:, slot, :])\
                    .then_inc(adj_stored[slot], 16)

            def load_masks(p, it):
                for u in range(RING):
                    n = tile_of(it, u)
                    sp.wait_ge(s["p_ready"], NT * p + n - RING + 1)
                    sp.dma_start(mask_w[:, u, :], adj8[ds(n * P, P), chunk(p) * CH // 4:(chunk(p) + 1) * CH // 4])\
                        .then_inc(mask_in[u], 16)

            def spread_den(p):
                sp.wait_ge(s["evacuated"], evacuations(p))
                for h in range(HP):
                    sp.dma_start(den_d[pair(p) * HP + h:pair(p) * HP + h + 1, chunk(p) * CH:(chunk(p) + 1) * CH],
                                 rden[D * h:D * h + 1, :]).then_inc(s["den_stored"], 16)
                sp.wait_ge(s["den_stored"], 32 * (p + 1))
                for h in range(HP):
                    src = den_d[pair(p) * HP + h, chunk(p) * CH:(chunk(p) + 1) * CH]
                    sp.dma_start(dsm[D * h:D * h + D, :], src.rearrange("(q c) -> q c", c=32))\
                        .then_inc(s["den_in"], 16)

            def spread_rec(p):
                sp.wait_ge(s["rec_made"], 2 * (p + 1))
                for h in range(HP):
                    dst = rec_d[pair(p) * HP + h, chunk(p) * CH:(chunk(p) + 1) * CH]
                    sp.dma_start(dst.rearrange("(q c) -> q c", c=32), rsm[D * h:D * h + D, :])\
                        .then_inc(s["rec_stored"], 16)
                sp.wait_ge(s["rec_stored"], 32 * (p + 1))
                load_rec(p)

            def load_rec(p):
                for h in range(HP):
                    src = rec_d[pair(p) * HP + h:pair(p) * HP + h + 1, chunk(p) * CH:(chunk(p) + 1) * CH]
                    sp.dma_start(rden[D * h:D * h + D, :], src.to_broadcast([D, CH])).then_inc(s["rden_in"], 16)

            for p in range(2 * PASSES):
                tiles = bring_adj if first_visit(p) else load_masks
                if p == 1:
                    for k in range(RING):
                        sp.wait_ge(adj_stored[k], 16 * ITS)
                if p == NB + 1:
                    for k in range(RING):
                        sp.wait_ge(adj_stored[k], 32 * ITS)
                tiles(p, 0)
                if p == 0:
                    store_f1(1)
                if 1 <= p <= PASSES:
                    spread_den(p - 1)
                if p == PASSES:
                    spread_rec(p - 1)
                if p > PASSES:
                    sp.wait_ge(s["agg_done"], p - 1)
                    load_rec(p - 1)
                tiles(p, 1)
                if 1 <= p < PASSES:
                    spread_rec(p - 1)
                if 1 <= p and p + 1 < 2 * PASSES:
                    sp.wait_ge(s["tanh_done"], NT * p)
                    load_f1(p + 1)
                with sp.Fori(2, ITS) as it:
                    tiles(p, it)
            sp.wait_ge(s["agg_done"], 2 * PASSES - 1)
            load_rec(2 * PASSES - 1)

            sp.wait_ge(s["e_used"], 2 * PASSES * NT)
            sp.dma_start(xn, x.rearrange("(t p) f -> p t f", p=P)).then_inc(s["xn_in"], 16)

            sp.wait_ge(s["agg_done"], 2 * PASSES)
            adj_v = adj8.rearrange("(t p) n -> p t n", p=P)

            def load_group(g, slot):
                sp.dma_start(adjg_w[:, slot, :, :], adj_v[:, :, ds(g * (GI // 4), GI // 4)]).then_inc(adjg_in[slot], 16)

            def store_group(g):
                for k in range(GT):
                    sp.wait_ge(s["y_ready"], GT * g + k + 1)
                    sp.dma_start(out[ds(g * GI + k * P, P), :], ybuf[:, k, :]).then_inc(out_free[k], 16)

            load_group(0, 0)
            load_group(1, 1)
            with sp.Fori(0, NG // 2 - 1) as gg:
                for v in range(2):
                    sp.wait_ge(s["u_full"], GT * (2 * gg + v + 1))
                    load_group(2 * gg + v + 2, v)
                    store_group(2 * gg + v)
            for g in range(NG - 2, NG):
                store_group(g)
            for k in range(GT):
                sp.wait_ge(out_free[k], 16 * NG + 16)

        @block.gpsimd
        def _(pool):
            pool.memset(wm[:, :, :], 0.0).then_inc(s["zeroed"], 1)
            pool.memset(wtbd[:, :, :], 0.0).then_inc(s["zeroed"], 1)
            pool.memset(vbd[:, :, :], 0.0).then_inc(s["zeroed"], 1)
            pool.memset(ident[:, :], 0.0).then_inc(s["ident_set"], 1)
            pool.wait_ge(s["ident_set"], 1)
            pool.affine_select(out=ident[:, :], in_=ident[:, :], compare_op=ALU.not_equal, fill=1.0,
                               base=0, pattern=[[-1, P]], channel_multiplier=1).then_inc(s["ident_set"], 1)
            pool.memset(vx[:, :, :, :], 1.0).then_inc(s["ones_set"], 1)
            pool.memset(ones16[:, :], 1.0).then_inc(s["ones_set"], 1)
            pool.memset(eps[:, 0:1], EPS_BN).then_inc(s["ones_set"], 1)
            pool.memset(eps[:, 1:2], EPS_LN).then_inc(s["ones_set"], 1)
            pool.wait_ge(s["ones_set"], 4)

            def steps(p, it):
                for u in range(RING):
                    n = tile_of(it, u)
                    m = NT * p + n
                    if not very_first(p, it):
                        pool.wait_ge(s["e_used"], m - RING + 1)
                    pool.tensor_copy(vx[:, u, :, 0:D],
                                     vals[:, ds(n, 1), pair(p) * P:(pair(p) + 1) * P]
                                     .rearrange("p a (h d) -> p (a h) d", h=HP)).then_inc(s["vx_ready"], 1)

            for p in range(2 * PASSES):
                if p == 0:
                    pool.wait_ge(s["xw_free"], NT)
                if p == PASSES:
                    pool.wait_ge(s["tr_copied"], NT // 2)
                steps(p, 0)
                with pool.Fori(1, ITS) as it:
                    steps(p, it)

        @block.scalar
        def _(act):
            def tanh(p, it, u):
                n = tile_of(it, u)
                m = NT * p + n
                if not very_first(p, it):
                    act.wait_ge(s["e_used"], m - RING + 1)
                elif u < 2:
                    act.wait_ge(s["xw_free"], n + 1)
                else:
                    act.wait_ge(s["xw_free"], NT)
                    act.wait_ge(s["f1_copied"], NC)
                for h in range(HP):
                    k = pair(p) * HP + h
                    last = act.activation(ering[:, u, h * CH:(h + 1) * CH], f1b[:, p % 2, h, :], ACT.Tanh,
                                          bias=f2h[:, ds(n, 1), k],
                                          scale=0.5)
                last.then_inc(s["tanh_done"], 1)

            def exp(p, n, slot):
                act.wait_ge(s["tanh_done"], NT * p + n + 1)
                act.activation(ering[:, slot, :], ering[:, slot, :], ACT.Exp, scale=0.5)\
                    .then_inc(s["e_ready"], 1)

            def steps(p, it):
                for u in range(RING):
                    tanh(p, it, u)
                    if not (very_first(p % PASSES, it) and u == 0):
                        exp(p, tile_of(it, u) - 1, (u - 1) % RING)

            def elu_parts(k, v, full, free, room, bank, tmp, slot, bias):
                act.wait_ge(s[full], k + 1)
                if not (isinstance(k, int) and k < 4):
                    act.wait_ge(s[room], k - 3)
                b = cols[:, v % 2, bias:bias + 1] if bias is not None else 0.0
                act.activation(tmp[:, 0, slot + v, :], ps[:, bank + v, :], ACT.Exp, bias=b)
                act.activation(tmp[:, 1, slot + v, :], ps[:, bank + v, :], ACT.Relu, bias=b).then_inc(s[free], 1)

            def bn_sqrt(k):
                act.wait_ge(s["bn_mv"], k + 1)
                act.activation(bnc[:, k, :, 0], mv[:, :, 1], ACT.Sqrt, bias=eps[:, 0:1]).then_inc(s["bn_sd"], 1)

            def encoder():
                def copy_transposed(c, v):
                    for q in range(2):
                        act.wait_ge(s["tr_full"], 2 * c + q + 1)
                        act.activation(vals[:, ds(4 * c + 2 * q, 2), :].rearrange("p a f -> p (a f)"),
                                       ps[:, 4 + 2 * v + q, :], ACT.Copy).then_inc(s["tr_copied"], 1)

                def piece(c, v):
                    for o in range(NB):
                        elu_parts(2 * c + o, 2 * v + o, "z_full", "z_free", "h_ready", 0, tmp_enc, 0, 2)

                for c in range(2):
                    piece(c, c)
                with act.Fori(1, NC // 2) as i:
                    for v in range(2):
                        piece(2 * i + v, v)
                        copy_transposed(2 * i + v - 2, v)
                for c in range(NC - 2, NC):
                    copy_transposed(c, c % 2)

            def decoder():
                def y_piece(c, v):
                    for o in range(NB):
                        elu_parts(2 * c + o, 2 * v + o, "y_full", "y_free", "yc_ready", 4, tmp_dec, 4, None)

                def z_piece(c, v):
                    for o in range(NB):
                        elu_parts(2 * NC + 2 * c + o, 2 * v + o, "z_full", "z_free", "h_ready", 0, tmp_dec, 0, 5)

                y_piece(0, 0)
                for c in range(2):
                    y_piece(c + 1, (c + 1) % 2)
                    z_piece(c, c)
                with act.Fori(1, NC // 2 - 1) as i:
                    for v in range(2):
                        y_piece(2 * i + v + 1, (v + 1) % 2)
                        z_piece(2 * i + v, v)
                y_piece(NC - 1, 1)
                z_piece(NC - 2, 0)
                z_piece(NC - 1, 1)

            def affine_out(c):
                for b in range(NB):
                    a = agg[:, b, c * BK:(c + 1) * BK]
                    act.activation(a, a, ACT.Identity, scale=bnc[:, 2, b, 1:2], bias=bnc[:, 2, b, 3:4])\
                        .then_inc(s["emb_ready"], 1)

            def ln_sqrt(g):
                act.wait_ge(s["ln_aggr"], 8 * (g + 1))
                act.activation(lnsd[:, 8 * g:8 * g + 8, 0], lnmv[:, 8 * g:8 * g + 8, 1], ACT.Sqrt,
                               bias=eps[:, 1:2]).then_inc(s["ln_sd"], 1)

            def hi(g):
                act.wait_ge(s["x1_done"], 8 * (g + 1))
                act.activation(x1s[:, 8 * g:8 * g + 8, 0:F], vals[:, 8 * g:8 * g + 8, :], ACT.Copy)\
                    .then_inc(s["hi_made"], 1)

            def lo(g):
                act.wait_ge(s["d_made"], g + 1)
                act.activation(x1s[:, 8 * g:8 * g + 8, F:2 * F], dtmp[:, 8 * (g % 2):8 * (g % 2) + 8, :],
                               ACT.Copy, scale=LO_SCALE).then_inc(s["lo_made"], 1)

            act.wait_ge(s["ones_set"], 4)
            for p in range(2 * PASSES):
                if p == PASSES:
                    exp(p - 1, NT - 1, RING - 1)
                act.wait_ge(f1_in[p % 2], 32 * (p // 2 + 1))
                steps(p, 0)
                if p == PASSES:
                    act.wait_ge(s["cols_in"], 16 * 8)
                    bn_sqrt(0)
                    encoder()
                    bn_sqrt(1)
                with act.Fori(1, ITS) as it:
                    steps(p, it)
            exp(2 * PASSES - 1, NT - 1, RING - 1)

            decoder()
            bn_sqrt(2)
            act.wait_ge(s["bn_step"], 4 * 3)
            for c in range(4):
                affine_out(c)
            ln_sqrt(0)
            affine_out(4)
            affine_out(5)
            ln_sqrt(1)
            hi(0)
            affine_out(6)
            affine_out(7)
            ln_sqrt(2)
            hi(1)
            lo(0)
            ln_sqrt(3)
            hi(2)
            lo(1)
            hi(3)
            lo(2)
            lo(3)

            with act.Fori(0, NG) as g:
                for k in range(GT):
                    act.wait_ge(s["u_full"], GT * g + k + 1)
                    act.activation(utmp[:, k, :], ps[:, k, F:2 * F], ACT.Copy, scale=1.0 / LO_SCALE)\
                        .then_inc(s["lo_scaled"], 1)
                    act.activation(degs[:, k, 0:1], ps[:, 4 + k, 0:1], ACT.Sqrt).then_inc(s["deg_sqrt"], 1)
                    act.wait_ge(s["y_step"], 3 * (GT * g + k) + 3)
                    act.activation(degs[:, k, 7:8], lnmv[:, k, 1:2], ACT.Sqrt, bias=eps[:, 1:2])\
                        .then_inc(s["y_sqrt"], 1)

        @block.vector
        def _(dve):
            dve.wait_ge(s["wv_done"], 1)
            dve.tensor_copy(wm[:, :, P:P + 2 * H],
                            ps[:, 0, 0:NB * 2 * H].rearrange("p (b c) -> p b c", b=NB)).then_inc(s["wv_copied"], 1)
            def f1_rows(c):
                for u in range(4):
                    dve.wait_ge(s["f1_full"], 4 * c + u + 1)
                    dve.tensor_copy(agg[0:H, 0, (4 * c + u) * BK:(4 * c + u + 1) * BK], ps[0:H, u, :])\
                        .then_inc(s["f1_copied"], 1)

            f1_rows(0)
            with dve.Fori(0, ITS) as it:
                for u in range(RING):
                    n = tile_of(it, u)
                    bank = ps[:, 4 + u, 0:NB * (P + 2 * H)].rearrange("p (b c) -> p b c", b=NB)
                    dve.wait_ge(s["xw_full"], n + 1)
                    dve.tensor_copy(vals[:, ds(n, 1), :].rearrange("p a (b c) -> p (a b) c", b=NB), bank[:, :, 0:P])
                    for b in range(NB):
                        last = dve.tensor_scalar(f2h[:, ds(n, 1), b * HP:(b + 1) * HP],
                                                 bank[:, b:b + 1, P + H + b * HP:P + H + (b + 1) * HP],
                                                 0.5, None, ALU.mult)
                    last.then_inc(s["xw_free"], 1)
            f1_rows(1)

            def masks(p, it, us=range(RING)):
                for u in us:
                    n = tile_of(it, u)
                    if first_visit(p):
                        dve.wait_ge(stage_in[u % 2], 16 * (visit(p) * NT // 2 + it * 2 + u // 2 + 1))
                        if not very_first(p, it):
                            dve.wait_ge(adj_stored[u], 16 * (visit(p) * ITS + it))
                        held(dve)
                        dve.tensor_copy(mask[:, u, :], stage[:, u % 2, :], saturate=False)\
                            .then_inc(s["mask_conv"], 1)
                        dve.wait_ge(s["mask_conv"], visit(p) * NT + n + 1)
                    else:
                        dve.wait_ge(mask_in[u], 16 * (reload(p) * ITS + it + 1))
                    dve.wait_ge(s["e_ready"], NT * p + n + 1)
                    held(dve)
                    e = ering[:, u, :].rearrange("p (h n) -> p h n", h=HP)
                    dve.tensor_tensor(e, e, mask[:, u:u + 1, :].to_broadcast([P, HP, CH]), ALU.mult)\
                        .then_inc(s["p_ready"], 1)

            def evacuate(p):
                dve.wait_ge(s["e_used"], NT * (p + 1))
                for h in range(HP):
                    rows = slice(D * h, D * h + D)
                    src = ps[0:D, 4 * h:4 * h + 4, :]
                    dve.tensor_copy(agg[rows, pair(p), chunk(p) * CH:(chunk(p) + 1) * CH]
                                    .rearrange("p (k n) -> p k n", k=4), src).then_inc(s["evacuated"], 1)
                    if p < PASSES:
                        dve.tensor_copy(rden[D * h:D * h + 1, :].rearrange("p (k n) -> p k n", k=4),
                                        ps[D:D + 1, 4 * h:4 * h + 4, :]).then_inc(s["evacuated"], 1)

            def reciprocals(p):
                dve.wait_ge(s["den_in"], 32 * (p + 1))
                dve.tensor_scalar(dsm[:, :], dsm[:, :], TINY, None, ALU.max).then_inc(s["rec_made"], 1)
                dve.wait_ge(s["rec_made"], 2 * p + 1)
                dve.reciprocal(rsm[:, :], dsm[:, :]).then_inc(s["rec_made"], 1)

            def normalise(p):
                dve.wait_ge(s["rden_in"], 32 * (p + 1))
                dve.wait_ge(s["evacuated"], evacuations(p))
                a = agg[:, pair(p), chunk(p) * CH:(chunk(p) + 1) * CH]
                if p < PASSES:
                    dve.tensor_tensor(a, a, rden[:, :], ALU.mult).then_inc(s["agg_done"], 1)
                    dve.wait_ge(s["agg_done"], p + 1)
                    for k in range(4):
                        c = chunk(p) * 4 + k
                        last = dve.bn_stats(stats[:, pair(p), c, :], agg[:, pair(p), c * BK:(c + 1) * BK])
                    return last
                dve.tensor_tensor(a, a, rden[:, :], ALU.mult).then_inc(s["scaled"], 1)
                dve.wait_ge(s["scaled"], p - PASSES + 1)
                dve.tensor_scalar(a, a, bnc[:, 1, pair(p), 1:2], bnc[:, 1, pair(p), 3:4], ALU.mult, ALU.add)\
                    .then_inc(s["agg_done"], 1)

            step = [0]

            def link(ins):
                step[0] += 1
                ins.then_inc(s["bn_step"], 1)
                dve.wait_ge(s["bn_step"], step[0])

            def bn_coefficients(k, gamma, beta):
                for b in range(NB):
                    last = dve.bn_aggr(mv[:, b, :], stats[:, b, :, :].rearrange("p c s -> p (c s)"))
                last.then_inc(s["bn_mv"], 1)
                dve.wait_ge(s["bn_mv"], k + 1)
                dve.wait_ge(s["bn_sd"], k + 1)
                c = bnc[:, k, :, :]
                link(dve.reciprocal(c[:, :, 1], c[:, :, 0]))
                link(dve.tensor_tensor(c[:, :, 1], c[:, :, 1], cols[:, :, gamma], ALU.mult))
                link(dve.tensor_tensor(c[:, :, 2], mv[:, :, 0], c[:, :, 1], ALU.mult))
                link(dve.tensor_tensor(c[:, :, 3], cols[:, :, beta], c[:, :, 2], ALU.subtract))

            def h_piece(base, c, v, tmp, src, dst):
                for o in range(NB):
                    k, slot = base + 2 * c + o, 2 * v + o
                    cc = ds(c * BK, BK)
                    e, r = tmp[:, 0, slot, :], tmp[:, 1, slot, :]
                    dve.wait_ge(s["z_free"], k + 1)
                    dve.scalar_tensor_tensor(out=r, in0=e, scalar=1.0, in1=r, op0=ALU.min, op1=ALU.add)\
                        .then_inc(s["elu_step"], 1)
                    dve.wait_ge(s["z_full"], base + 2 * c + 2)
                    dve.wait_ge(s["elu_step"], 2 * k + 1)
                    dve.scalar_tensor_tensor(out=dst[:, o, cc], in0=r, scalar=-1.0, in1=src[:, o, cc],
                                             op0=ALU.add, op1=ALU.add).then_inc(s["elu_step"], 1)
                    dve.wait_ge(s["elu_step"], 2 * k + 2)
                    dve.bn_stats(stats[:, o, ds(c, 1), :], dst[:, o, cc]).then_inc(s["h_ready"], 1)

            def yc_piece(c, v):
                for o in range(NB):
                    k, slot = 2 * c + o, 4 + 2 * v + o
                    e, r = tmp_dec[:, 0, slot, :], tmp_dec[:, 1, slot, :]
                    dve.wait_ge(s["y_free"], k + 1)
                    dve.scalar_tensor_tensor(out=r, in0=e, scalar=1.0, in1=r, op0=ALU.min, op1=ALU.add)\
                        .then_inc(s["y_step0"], 1)
                    dve.wait_ge(s["y_step0"], k + 1)
                    dve.tensor_scalar(yc[:, o, ds(c * BK, BK)], r, -1.0, None, ALU.add).then_inc(s["yc_ready"], 1)

            def encoder():
                bn_coefficients(0, 0, 1)
                for cc in (slice(0, BK), slice(BK, N)):
                    for b in range(NB):
                        dve.tensor_scalar(agg[:, b, cc], agg[:, b, cc], bnc[:, 0, b, 1:2], bnc[:, 0, b, 3:4],
                                          ALU.mult, ALU.add).then_inc(s["xn_ready"], 1)
                dve.wait_ge(s["xn_ready"], 2 * NB)
                with dve.Fori(0, NC // 2) as i:
                    for v in range(2):
                        h_piece(0, 2 * i + v, v, tmp_enc, agg, agg)
                dve.wait_ge(s["h_ready"], 2 * NC)
                bn_coefficients(1, 3, 4)

            for p in range(2 * PASSES):
                if p == PASSES:
                    evacuate(p - 1)
                    masks(p, 0, (0, 1))
                    reciprocals(p - 1)
                    masks(p, 0, (2,))
                    normalise(p - 1).then_inc(s["stats_done"], 1)
                    dve.wait_ge(s["stats_done"], 1)
                    dve.wait_ge(s["cols_in"], 16 * 8)
                    encoder()
                    masks(p, 0, (3,))
                elif p:
                    masks(p, 0, (0,))
                    evacuate(p - 1)
                    masks(p, 0, (1, 2, 3))
                else:
                    masks(p, 0)
                if 1 <= p < PASSES:
                    reciprocals(p - 1)
                masks(p, 1)
                masks(p, 2)
                if 1 <= p and p != PASSES:
                    normalise(p - 1)
                with dve.Fori(3, ITS) as it:
                    masks(p, it)
            evacuate(2 * PASSES - 1)
            normalise(2 * PASSES - 1)

            yc_piece(0, 0)
            with dve.Fori(0, NC // 2 - 1) as i:
                for v in range(2):
                    yc_piece(2 * i + v + 1, (v + 1) % 2)
                    h_piece(2 * NC, 2 * i + v, v, tmp_dec, yc, agg)
            yc_piece(NC - 1, 1)
            h_piece(2 * NC, NC - 2, 0, tmp_dec, yc, agg)
            h_piece(2 * NC, NC - 1, 1, tmp_dec, yc, agg)
            dve.wait_ge(s["h_ready"], 4 * NC)
            bn_coefficients(2, 6, 7)

            def sums(g):
                def tile_stats(j):
                    dve.wait_ge(s["sum_ready"], j + 1)
                    for t in range(2 * j, 2 * j + 2):
                        last = dve.bn_stats(lnst[:, t, :], vals[:, t, :])
                    return last

                for j in range(4 * g, 4 * g + 4):
                    dve.wait_ge(s["tr_full"], 2 * NC + j + 1)
                    dve.tensor_tensor(vals[:, 2 * j:2 * j + 2, :].rearrange("p a f -> p (a f)"), ps[:, j % 8, :],
                                      xn[:, 2 * j:2 * j + 2, :].rearrange("p a f -> p (a f)"), ALU.add)\
                        .then_inc(s["sum_ready"], 1)
                    if j > 4 * g:
                        tile_stats(j - 1)
                link(tile_stats(4 * g + 3))
                for t in range(8 * g, 8 * g + 8):
                    dve.bn_aggr(lnmv[:, t, :], lnst[:, t, :]).then_inc(s["ln_aggr"], 1)

            def norm(g):
                dve.wait_ge(s["ln_sd"], g + 1)
                t8 = slice(8 * g, 8 * g + 8)
                dve.reciprocal(lnsd[:, t8, 1], lnsd[:, t8, 0]).then_inc(s["ln_rec"], 1)
                dve.wait_ge(s["ln_rec"], g + 1)
                dve.wait_ge(s["ln_aggr"], 8 * (g + 1))
                for t in range(8 * g, 8 * g + 8):
                    dve.tensor_scalar(vals[:, t, :], vals[:, t, :], lnmv[:, t, 0:1], lnsd[:, t, 1:2],
                                      ALU.subtract, ALU.mult).then_inc(s["x1_done"], 1)

            def rest(g):
                t8 = slice(8 * g, 8 * g + 8)
                dve.wait_ge(s["hi_made"], g + 1)
                if g >= 2:
                    dve.wait_ge(s["lo_made"], g - 1)
                dve.tensor_tensor(dtmp[:, 8 * (g % 2):8 * (g % 2) + 8, :], vals[:, t8, :], x1s[:, t8, 0:F],
                                  ALU.subtract).then_inc(s["d_made"], 1)

            dve.wait_ge(s["xn_in"], 16)
            sums(0)
            sums(1)
            norm(0)
            sums(2)
            norm(1)
            rest(0)
            sums(3)
            norm(2)
            rest(1)
            norm(3)
            rest(2)
            rest(3)

            for k in range(GT):
                dve.memset(ybuf[:, k, 0:1], 0.0).then_inc(out_free[k], 16)
            dve.memset(degs[:, :, :], 0.0).then_inc(s["u_free"], GT)
            with dve.Fori(0, NG) as g:
                for k in range(GT):
                    r = GT * g + k
                    d = degs[:, k, :]
                    dve.wait_ge(s["lo_scaled"], r + 1)
                    dve.tensor_tensor(utmp[:, k, :], ps[:, k, 0:F], utmp[:, k, :], ALU.add)\
                        .then_inc(s["deg_step"], 1)
                    dve.wait_ge(s["deg_sqrt"], r + 1)
                    dve.tensor_copy(d[:, 1:2], ps[:, 4 + k, 0:1]).then_inc(s["u_free"], 1)
                    dve.tensor_scalar(d[:, 2:3], d[:, 0:1], EPS_NORM, None, ALU.max).then_inc(s["deg_step"], 1)
                    dve.wait_ge(s["deg_step"], 7 * r + 2)
                    dve.reciprocal(d[:, 3:4], d[:, 2:3]).then_inc(s["deg_step"], 1)
                    dve.wait_ge(s["deg_step"], 7 * r + 3)
                    dve.tensor_scalar(d[:, 4:5], d[:, 3:4], 1.0, None, ALU.add).then_inc(s["deg_step"], 1)
                    dve.wait_ge(s["deg_step"], 7 * r + 4)
                    dve.wait_ge(s["u_free"], GT + r + 1)
                    dve.tensor_tensor(d[:, 5:6], d[:, 4:5], d[:, 1:2], ALU.mult).then_inc(s["deg_step"], 1)
                    dve.wait_ge(s["deg_step"], 7 * r + 5)
                    dve.reciprocal(d[:, 6:7], d[:, 5:6]).then_inc(s["deg_step"], 1)
                    dve.wait_ge(s["deg_step"], 7 * r + 6)
                    dve.tensor_tensor(d[:, 6:7], d[:, 6:7], d[:, 4:5], ALU.mult).then_inc(s["deg_step"], 1)
                    dve.wait_ge(s["deg_step"], 7 * r + 7)
                    dve.scalar_tensor_tensor(out=utmp[:, k, :], in0=utmp[:, k, :], scalar=d[:, 6:7],
                                             in1=vals[:, ds(r, 1), :].rearrange("p a f -> p (a f)"),
                                             op0=ALU.mult, op1=ALU.add).then_inc(s["y_step"], 1)
                    dve.wait_ge(s["y_step"], 3 * r + 1)
                    dve.bn_stats(lnst[:, k, :], utmp[:, k, :]).then_inc(s["y_step"], 1)
                    dve.wait_ge(s["y_step"], 3 * r + 2)
                    held(dve)
                    dve.bn_aggr(lnmv[:, k, :], lnst[:, k, :]).then_inc(s["y_step"], 1)
                    dve.wait_ge(s["y_sqrt"], r + 1)
                    dve.reciprocal(lnsd[:, k, 1:2], degs[:, k, 7:8]).then_inc(s["fin_step"], 1)
                    dve.wait_ge(s["fin_step"], r + 1)
                    dve.wait_ge(out_free[k], 16 * g + 16)
                    dve.tensor_scalar(ybuf[:, k, :], utmp[:, k, :], lnmv[:, k, 0:1], lnsd[:, k, 1:2],
                                      ALU.subtract, ALU.mult).then_inc(s["y_ready"], 1)

        @block.tensor
        def _(pe):
            pe.wait_ge(s["w_in"], 16 * 4 * H)
            for b in range(NB):
                last = pe.matmul(ps[:, 0, b * 2 * H:(b + 1) * 2 * H], wtbd[:, b, :], vbd[:, b, :],
                                 start=True, stop=True)
            last.then_inc(s["wv_done"], 1)
            pe.wait_ge(s["wv_copied"], 1)


            def f1_rows(c):
                if c >= 4:
                    pe.wait_ge(s["f1_copied"], c - 3)
                if c % 2 == 0:
                    pe.wait_ge(x_in[c // 2], 16)
                for b in range(NB):
                    last = pe.matmul(ps[0:H, c % 4, :], wm[:, b, P:P + H], xTs[:, b, c * BK:(c + 1) * BK],
                                     start=(b == 0), stop=(b == NB - 1))
                last.then_inc(s["f1_full"], 1)

            for c in range(4):
                f1_rows(c)
            for n in range(NT):
                if n >= RING:
                    pe.wait_ge(s["xw_free"], n - RING + 1)
                if n % 8 == 0:
                    pe.wait_ge(x_in[n // 8], 16)
                for b in range(NB):
                    last = pe.matmul(ps[:, 4 + n % RING, b * (P + 2 * H):(b + 1) * (P + 2 * H)],
                                     xTs[:, b, n * P:(n + 1) * P], wm[:, b, :], start=True, stop=True)
                last.then_inc(s["xw_full"], 1)
            for c in range(4, NC):
                f1_rows(c)
            pe.wait_ge(s["xw_free"], NT)
            pe.wait_ge(s["f1_copied"], NC)

            def steps(p, it):
                for u in range(RING):
                    n = tile_of(it, u)
                    m = NT * p + n
                    fixed = isinstance(it, int)
                    start, stop = fixed and it == 0 and u == 0, fixed and it == ITS - 1 and u == RING - 1
                    pe.wait_ge(s["vx_ready"], m + 1)
                    pe.wait_ge(s["p_ready"], m + 1)
                    for h in range(HP):
                        if start and p % PASSES:
                            before = evacuations(p - 1) - evacuations(p - 2) if p > 1 else 4
                            pe.wait_ge(s["evacuated"], evacuations(p - 1) - (HP - 1 - h) * before // HP)
                        for c in range(4):
                            last = pe.matmul(ps[0:D + 1, 4 * h + c, :], vx[:, u, h, :],
                                             ering[:, u, h * CH + c * BK:h * CH + (c + 1) * BK],
                                             start=start, stop=stop)
                    last.then_inc(s["e_used"], 1)

            def z_chunk(w, src, c, base):
                for o in range(NB):
                    k = base + 2 * c + o
                    if k >= 4:
                        pe.wait_ge(s["z_free"], k - 3)
                    for b in range(NB):
                        last = pe.matmul(ps[:, k % 4, :], w[:, b, o * P:(o + 1) * P],
                                         src[:, b, c * BK:(c + 1) * BK], start=(b == 0), stop=(b == NB - 1))
                    last.then_inc(s["z_full"], 1)

            def transposes(c, bank):
                for q in range(2):
                    for t in range(2):
                        for b in range(NB):
                            n = 4 * c + 2 * q + t
                            last = pe.transpose(ps[:, bank + q, t * F + b * P:t * F + (b + 1) * P],
                                                agg[:, b, n * P:(n + 1) * P], ident[:, :])
                    last.then_inc(s["tr_full"], 1)

            for p in range(2 * PASSES):
                if p == PASSES:
                    pe.wait_ge(s["mlp_in"], 32)
                    pe.wait_ge(s["ident_set"], 2)
                    pe.wait_ge(s["evacuated"], evacuations(p - 1))
                    for c in range(NC + 2):
                        if c < NC:
                            pe.wait_ge(s["xn_ready"], NB if c == 0 else 2 * NB)
                            z_chunk(wenc, agg, c, 0)
                        if c >= 2:
                            pe.wait_ge(s["h_ready"], 2 * (c - 1))
                            if c >= 4:
                                pe.wait_ge(s["tr_copied"], 2 * (c - 3))
                            transposes(c - 2, 4 + 2 * (c % 2))
                    pe.wait_ge(s["tr_copied"], 2 * NC)
                steps(p, 0)
                with pe.Fori(1, ITS - 1) as it:
                    steps(p, it)
                steps(p, ITS - 1)

            def y_chunk(c):
                pe.wait_ge(s["agg_done"], 2 * PASSES if c >= NC // NCH else 2 * PASSES - NB)
                for o in range(NB):
                    k = 2 * c + o
                    if k >= 4:
                        pe.wait_ge(s["y_free"], k - 3)
                    pe.matmul(ps[:, 4 + k % 4, :], wtbd[:, o, :], agg[:, o, c * BK:(c + 1) * BK],
                              start=True, stop=True).then_inc(s["y_full"], 1)

            pe.wait_ge(s["evacuated"], evacuations(2 * PASSES - 1))
            y_chunk(0)
            y_chunk(1)
            for c in range(NC):
                pe.wait_ge(s["yc_ready"], 2 * c + 2)
                z_chunk(wdec, yc, c, 2 * NC)
                if c + 2 < NC:
                    y_chunk(c + 2)
            pe.wait_ge(s["z_free"], 4 * NC)
            pe.wait_ge(s["y_free"], 2 * NC)
            for c in range(NC):
                pe.wait_ge(s["emb_ready"], 2 * c + 2)
                if c >= 4:
                    pe.wait_ge(s["sum_ready"], 2 * (c - 3))
                transposes(c, 2 * (c % 4))

            with pe.Fori(0, NG // 2) as gg:
                for v in range(2):
                    g = 2 * gg + v
                    pe.wait_ge(adjg_in[v], 16 * (gg + 1))
                    for k in range(GT):
                        pe.wait_ge(s["u_free"], GT * g + k + 1)
                        held(pe)
                        for t in range(NT):
                            if k == 0 and t % 8 == 0:
                                pe.wait_ge(s["lo_made"], t // 8 + 1)
                            w = adjg[:, v, t, k * P:(k + 1) * P]
                            pe.matmul(ps[:, 4 + k, 0:2], w, ones16[:, :], start=(t == 0), stop=(t == NT - 1))
                            last = pe.matmul(ps[:, k, :], w, x1s[:, t, :], start=(t == 0), stop=(t == NT - 1))
                        last.then_inc(s["u_full"], 1)


def kernel(x, adj, L0_gnn_W, L0_gnn_V, L0_gnn_enc_bn_gamma, L0_gnn_enc_bn_beta, L0_gnn_enc_mlp_W,
           L0_gnn_enc_mlp_b, L0_gnn_enc_mlp_bn_gamma, L0_gnn_enc_mlp_bn_beta, L0_gnn_dec_mlp_W,
           L0_gnn_dec_mlp_b, L0_gnn_dec_mlp_bn_gamma, L0_gnn_dec_mlp_bn_beta):
    import numpy as np
    import concourse.bacc as bacc
    from concourse.bass_utils import run_bass_kernel_spmd

    x, adj, W = np.asarray(x), np.asarray(adj), np.asarray(L0_gnn_W)
    host = {
        "xT": x.T, "x": x, "adjT": adj.T, "W": W, "WT": W.transpose(0, 2, 1), "V": L0_gnn_V,
        "enc_g": L0_gnn_enc_bn_gamma, "enc_b": L0_gnn_enc_bn_beta,
        "encm_WT": np.asarray(L0_gnn_enc_mlp_W).T, "encm_bias": L0_gnn_enc_mlp_b,
        "encm_g": L0_gnn_enc_mlp_bn_gamma, "encm_b": L0_gnn_enc_mlp_bn_beta,
        "decm_WT": np.asarray(L0_gnn_dec_mlp_W).T, "decm_bias": L0_gnn_dec_mlp_b,
        "decm_g": L0_gnn_dec_mlp_bn_gamma, "decm_b": L0_gnn_dec_mlp_bn_beta,
    }
    nc = bacc.Bacc("TRN2", target_bir_lowering=False, num_devices=1)
    arrays, args = {}, []
    for name, a in host.items():
        a = np.ascontiguousarray(a)
        arrays[f"in_{name}"] = a
        args.append(nc.dram_tensor(f"in_{name}", a.shape, mybir.dt.from_np(a.dtype), kind="ExternalInput").ap())
    out = nc.dram_tensor("out", [N, F], F32, kind="ExternalOutput").ap()
    build(nc, *args, out)
    r = run_bass_kernel_spmd(nc, [arrays], core_ids=[0])
    return r.results[0]["out"]
```

```python
from contextlib import ExitStack

import concourse.bass as bass
from concourse import mybir

ALU = mybir.AluOpType
ACT = mybir.ActivationFunctionType
F32 = mybir.dt.float32
F16 = mybir.dt.float16
F8 = mybir.dt.float8e4
ds = bass.ds

P = 128
N = 4096
F = 256
H = 4
D = F // H
NT = N // P
NB = F // P
HP = 2
CH = 2048
NCH = N // CH
BK = 512
NC = N // BK
PASSES = NCH * NB
RING = 4
CYCLE = 8
ITS = NT // CYCLE
EPS_BN = 1e-6
EPS_LN = 1e-5
EPS_NORM = 1e-12
TINY = 1e-30
SCALE = 2048.0
KEPT = [1, 5]
SPLIT = [2, 6]
MADE = [u for u in range(CYCLE) if u not in KEPT]
ALL = list(range(CYCLE))
GI = 512
NG = N // GI
GT = GI // P


def build(nc, xT, x, adjT, W, WT, V, enc_g, enc_b, encm_WT, encm_bias, encm_g, encm_b,
          decm_WT, decm_bias, decm_g, decm_b, out):
    adj8 = nc.dram_tensor("adj8", [N, N // 4], F32, kind="Internal").ap()
    f1_d = nc.dram_tensor("f1_d", [H, N], F32, kind="Internal").ap()
    e_d = nc.dram_tensor("e_d", [PASSES * ITS * len(KEPT) * P, 2 * HP * CH], F16, kind="Internal").ap()
    den_d = nc.dram_tensor("den_d", [H, N], F32, kind="Internal").ap()
    rec_d = nc.dram_tensor("rec_d", [H, N], F32, kind="Internal").ap()

    with ExitStack() as ctx:
        def sb(name, shape, dt=F32):
            return ctx.enter_context(nc.sbuf_tensor(name, shape, dt))

        def sem(name):
            return ctx.enter_context(nc.semaphore(name))

        vals = sb("vals", [P, NT, F])
        agg = sb("agg", [P, NB, N])
        ering = sb("ering", [P, RING, HP * CH])
        f1b = sb("f1b", [P, 2, HP, CH])
        io = sb("io", [P, 8192])
        vx = sb("vx", [P, RING, HP, P])
        vx16 = sb("vx16", [P, RING, 2 * P], F16)
        vd = sb("vd", [P, P])
        wm = sb("wm", [P, NB, P + 2 * H])
        wtbd = sb("wtbd", [P, NB, P])
        vbd = sb("vbd", [P, NB, 2 * H])
        wenc = sb("wenc", [P, NB, F])
        wdec = sb("wdec", [P, NB, F])
        cols = sb("cols", [P, NB, 8])
        f2h = sb("f2h", [P, NT, H])
        dsm = sb("dsm", [P, 32])
        rsm = sb("rsm", [P, 32])
        ident = sb("ident", [P, P])
        ones16 = sb("ones16", [P, 2], F16)
        eps = sb("eps", [P, 2])
        stats = sb("stats", [P, NB, NC, 6])
        mv = sb("mv", [P, NB, 2])
        bnc = sb("bnc", [P, 3, NB, 4])
        lnst = sb("lnst", [P, NT, 6])
        lnmv = sb("lnmv", [P, NT, 2])
        lnsd = sb("lnsd", [P, NT, 2])
        degs = dsm[:, :].rearrange("p (c k) -> p c k", k=GT)
        ps = ctx.enter_context(nc.psum_tensor("ps", [P, 8, BK], F32))

        mask_w = io[:, 0:RING * CH // 4].rearrange("p (s n) -> p s n", s=RING)
        mask = io[:, 0:RING * CH // 4].bitcast(F8).rearrange("p (s n) -> p s n", s=RING)
        stage = io[:, 2048:6144].rearrange("p (s n) -> p s n", s=2)
        rden = io[:, 6144:8192]
        adjg_w = io[:, :].rearrange("p (s t n) -> p s t n", s=2, t=NT)
        adjg = io[:, :].bitcast(F8).rearrange("p (s t n) -> p s t n", s=2, t=NT)
        ering16 = ering[:, :, :].bitcast(F16)
        split16 = io[:, 2048:6144].bitcast(F16)
        xTs = ering[:, 2:4, :]
        f1row = agg[0:H, 0, :]
        tmp_enc = io[:, 2048:6144].rearrange("p (a k n) -> p a k n", a=2, n=BK)
        tmp_dec = f1b[:, :, :, :].rearrange("p a h (k n) -> p a (h k) n", n=BK)
        yc = ering[:, 0:2, :]
        xn = ering[:, 2:4, :].rearrange("p a (t f) -> p (a t) f", f=F)
        x1s = ering[:, 0:2, :].bitcast(F16).rearrange("p a (t c) -> p (a t) c", c=2 * F)
        dtmp = f1b[:, 0, :, :].rearrange("p h (k f) -> p (h k) f", f=F)
        utmp = f1b[:, 1, :, :].rearrange("p h (k f) -> p (h k) f", f=F)
        fold1 = ering[:, 2, 0:2048].bitcast(F8).rearrange("p (t n) -> p t n", n=GI)
        fold2 = ering[:, 2, 2048:4096].bitcast(F8).rearrange("p (v t n) -> p v t n", v=2, n=GI)
        ybuf = agg[:, 0, :].rearrange("p (k f) -> p k f", f=F)

        s = {k: sem(k) for k in (
            "zeroed", "wt_in", "w_in", "mlp_in", "cols_in", "ident_set", "ones_set",
            "wv_done", "wv_copied", "xw_full", "xw_free", "f1_full", "f1_copied", "f1_stored",
            "tanh_done", "e_ready", "p_ready", "e_used", "vx_ready", "mask_conv",
            "evacuated", "den_stored", "den_in", "rec_made", "rec_stored", "rden_in", "agg_done",
            "stats_done", "split_step", "hi_split", "lo_split", "hi_stored", "lo_stored", "split_done", "vx_zero", "v_step",
            "em_ready", "u_step",
            "bn_mv", "bn_sd", "bn_step", "xn_ready",
            "z_full", "z_free", "elu_step", "y_step0",
            "h_ready", "y_full", "y_free", "yc_ready", "tr_full", "tr_copied", "emb_ready",
            "xn_in", "sum_ready", "ln_aggr", "ln_sd", "ln_rec", "x1_done", "hi_made",
            "d_made", "lo_made", "u_full", "u_free", "lo_scaled", "fold_step", "folded", "deg_full", "deg_step", "deg_sqrt", "y_step",
            "y_sqrt", "y_ready", "fin_step", "held")}
        e_loaded = [sem(f"e_loaded{k}") for k in range(RING)]
        x_in = [sem(f"x_in{k}") for k in range(4)]
        f1_in = [sem(f"f1_in{b}") for b in range(2)]
        mask_in = [sem(f"mask_in{k}") for k in range(RING)]
        stage_in = [sem(f"stage_in{k}") for k in range(2)]
        adj_stored = [sem(f"adj_stored{k}") for k in range(RING)]
        adjg_in = [sem(f"adjg_in{k}") for k in range(2)]
        out_free = [sem(f"out_free{k}") for k in range(GT)]

        def first_visit(p):
            return p in (0, NB)

        def visit(p):
            return sum(first_visit(q) for q in range(p))

        def reload(p):
            return p - visit(p)

        def chunk(p):
            return (p % PASSES) // NB

        def pair(p):
            return p % NB

        def tile_of(it, u):
            return it * CYCLE + u

        def first_it(it):
            return isinstance(it, int) and it == 0

        def very_first(p, it, u):
            return p == 0 and first_it(it) and u < RING

        def computed(p):
            return ALL if p < PASSES else MADE

        def in_slot(p, u):
            return [v for v in computed(p) if v % RING == u % RING]

        def made(p, it, u):
            if p < PASSES:
                return NT * p + tile_of(it, u) + 1
            return NT * PASSES + len(MADE) * (ITS * (p - PASSES) + it) + MADE.index(u) + 1

        def kept(p, it, u):
            return len(KEPT) * (ITS * (p % PASSES) + it) + KEPT.index(u) + 1

        def splits(p, it, u):
            return len(SPLIT) * (ITS * (p - PASSES) + it) + SPLIT.index(u) + 1

        def loads(p, it, u):
            if p < PASSES:
                return reload(p) * NT // RING + it * CYCLE // RING + u // RING + 1
            us = in_slot(p, u)
            return reload(PASSES) * NT // RING + len(us) * (ITS * (p - PASSES) + it) + us.index(u) + 1

        def loaded(p, it, u):
            us = [v for v in KEPT if v % RING == u % RING]
            return len(us) * (ITS * (p - PASSES) + it) + us.index(u) + 1

        def before(p, it, u, us=None):
            mine = us(p, u) if us else [u % RING, u % RING + RING]
            if mine.index(u):
                return p, it, mine[mine.index(u) - 1]
            if first_it(it):
                return p - 1, ITS - 1, (us(p - 1, u) if us else mine)[-1]
            return p, it - 1, mine[-1]

        def halves(tiles, h=HP - 1):
            return HP * (tiles - 1) + h + 1

        def hi_lo(p):
            if p < PASSES - 1:
                return agg[:, 0, CH:N].bitcast(F16), agg[:, 1, CH:N].bitcast(F16)
            return stage[:, 0, :].bitcast(F16), stage[:, 1, :].bitcast(F16)

        def evacuations(p):
            return 4 * (p + 1) if p < PASSES else 4 * PASSES + 2 * (p + 1 - PASSES)

        def deg_psum(v):
            return ps[:, 4 + v, 0:2 * GT].rearrange("p (k c) -> p k c", c=2)[:, :, 0]

        def held(eng):
            eng.sem_inc(s["held"], 1)

        block = ctx.enter_context(nc.Block())

        @block.sync
        def _(sp):
            def load_x(k):
                c = slice(k * N // 4, (k + 1) * N // 4)
                sp.dma_start(xTs[:, :, c], xT.rearrange("(b p) n -> p b n", p=P)[:, :, c]).then_inc(x_in[k], 16)

            load_x(0)
            load_x(1)
            sp.wait_ge(s["zeroed"], 3)
            with nc.allow_non_contiguous_dma(reason="single columns of the small V"):
                for h in range(H):
                    rows, b, c = slice(D * (h % 2), D * (h % 2) + D), h // 2, D * (h % 2)
                    sp.dma_start(wtbd[rows, b, c:c + D], WT[h]).then_inc(s["wt_in"], 16)
                    sp.dma_start(vbd[rows, b, :].rearrange("p (k h) -> p k h", h=H)[:, :, h],
                                 V[h].rearrange("k d o -> d (k o)")).then_inc(s["wt_in"], 16)
                for h in range(H):
                    rows, b, c = slice(D * (h % 2), D * (h % 2) + D), h // 2, D * (h % 2)
                    sp.dma_start(wm[rows, b, c:c + D], W[h]).then_inc(s["w_in"], 16)
                load_x(2)
                load_x(3)
                for k, v in enumerate((enc_g, enc_b, encm_bias, encm_g, encm_b, decm_bias, decm_g, decm_b)):
                    sp.dma_start(cols[:, :, k], v.rearrange("(b p) -> p b", p=P)).then_inc(s["cols_in"], 16)
            sp.dma_start(wenc[:, :, :], encm_WT.rearrange("(b p) o -> p b o", p=P)).then_inc(s["mlp_in"], 16)
            sp.dma_start(wdec[:, :, :], decm_WT.rearrange("(b p) o -> p b o", p=P)).then_inc(s["mlp_in"], 16)

            def store_f1(c):
                sp.wait_ge(s["f1_copied"], (c + 1) * NC // NCH)
                sp.dma_start(f1_d[:, c * CH:(c + 1) * CH], f1row[:, c * CH:(c + 1) * CH])\
                    .then_inc(s["f1_stored"], 16)
                sp.wait_ge(s["f1_stored"], 16 * (c + 1))

            def load_f1(p):
                for h in range(HP):
                    src = f1_d[pair(p) * HP + h:pair(p) * HP + h + 1, chunk(p) * CH:(chunk(p) + 1) * CH]
                    sp.dma_start(f1b[:, p % 2, h, :], src.to_broadcast([P, CH])).then_inc(f1_in[p % 2], 16)

            def next_f1(p):
                if p == 0:
                    load_f1(1)
                elif p + 1 < 2 * PASSES:
                    sp.wait_ge(s["tanh_done"], halves(made(p - 1, ITS - 1, CYCLE - 1)))
                    load_f1(p + 1)

            store_f1(0)
            load_f1(0)

            def load_adj(p, it, u):
                sp.dma_start(stage[:, u % 2, :], adjT[ds(tile_of(it, u) * P, P), chunk(p) * CH:(chunk(p) + 1) * CH])\
                    .then_inc(stage_in[u % 2], 16)

            def bring_adj(p, it, us=ALL):
                if first_it(it) and us[0] == 0:
                    load_adj(p, 0, 0)
                    load_adj(p, 0, 1)
                    if p == 0:
                        store_f1(1)
                for u in us:
                    n = tile_of(it, u)
                    sp.wait_ge(s["mask_conv"], visit(p) * NT + n + 1)
                    if not (isinstance(it, int) and it == ITS - 1 and u + 2 >= CYCLE):
                        load_adj(p, it, u + 2)
                    sp.dma_start(adj8[ds(n * P, P), chunk(p) * CH // 4:(chunk(p) + 1) * CH // 4],
                                 mask_w[:, u % RING, :]).then_inc(adj_stored[u % RING], 16)
                    if u - 1 in KEPT:
                        store_e(p, it, u - 1)

            def load_masks(p, it, us=ALL):
                for u in us:
                    n = tile_of(it, u)
                    if u in computed(p):
                        if first_visit(p - 1) and first_it(it) and u < RING:
                            sp.wait_ge(adj_stored[u], 16 * visit(p) * NT // RING)
                        sp.wait_ge(s["p_ready"], halves(made(*before(p, it, u, in_slot))))
                        sp.dma_start(mask_w[:, u % RING, :],
                                     adj8[ds(n * P, P), chunk(p) * CH // 4:(chunk(p) + 1) * CH // 4])\
                            .then_inc(mask_in[u % RING], 16)
                    else:
                        load_e(p, it, u)
                    if p < PASSES:
                        if u - RING in KEPT:
                            store_e(p, it, u - RING)
                        if u == CYCLE - 1:
                            for v in KEPT:
                                if v >= RING:
                                    store_e(p, it, v)

            def store_e(p, it, u):
                k = kept(p, it, u)
                for a, (made_it, stored) in enumerate((("hi_split", "hi_stored"), ("lo_split", "lo_stored"))):
                    sp.wait_ge(s[made_it], k)
                    sp.dma_start(e_d[ds((k - 1) * P, P), a * HP * CH:(a + 1) * HP * CH], hi_lo(p)[a])\
                        .then_inc(s[stored], 16)

            def load_e(p, it, u):
                sp.wait_ge(s["e_used"], halves(NT * p + tile_of(it, u) - RING + 1))
                sp.dma_start(ering16[:, u % RING, :], e_d[ds((kept(p, it, u) - 1) * P, P), :])\
                    .then_inc(e_loaded[u % RING], 16)

            def spread_den(p):
                sp.wait_ge(s["evacuated"], evacuations(p))
                for h in range(HP):
                    sp.dma_start(den_d[pair(p) * HP + h:pair(p) * HP + h + 1, chunk(p) * CH:(chunk(p) + 1) * CH],
                                 rden[D * h:D * h + 1, :]).then_inc(s["den_stored"], 16)
                sp.wait_ge(s["den_stored"], 32 * (p + 1))
                for h in range(HP):
                    src = den_d[pair(p) * HP + h, chunk(p) * CH:(chunk(p) + 1) * CH]
                    sp.dma_start(dsm[D * h:D * h + D, :], src.rearrange("(q c) -> q c", c=32))\
                        .then_inc(s["den_in"], 16)

            def spread_rec(p):
                sp.wait_ge(s["rec_made"], 2 * (p + 1))
                for h in range(HP):
                    dst = rec_d[pair(p) * HP + h, chunk(p) * CH:(chunk(p) + 1) * CH]
                    sp.dma_start(dst.rearrange("(q c) -> q c", c=32), rsm[D * h:D * h + D, :])\
                        .then_inc(s["rec_stored"], 16)
                sp.wait_ge(s["rec_stored"], 32 * (p + 1))
                load_rec(p)

            def load_rec(p):
                for h in range(HP):
                    src = rec_d[pair(p) * HP + h:pair(p) * HP + h + 1, chunk(p) * CH:(chunk(p) + 1) * CH]
                    sp.dma_start(rden[D * h:D * h + D, :], src.to_broadcast([D, CH])).then_inc(s["rden_in"], 16)

            for p in range(2 * PASSES):
                tiles = bring_adj if first_visit(p) else load_masks
                if p == PASSES:
                    tiles(p, 0, [u for u in MADE if u < RING])
                    spread_den(p - 1)
                    spread_rec(p - 1)
                    for stored in ("hi_stored", "lo_stored"):
                        sp.wait_ge(s[stored], 16 * kept(p - 1, ITS - 1, KEPT[-1]))
                    tiles(p, 0, [u for u in KEPT if u < RING])
                    next_f1(p)
                    tiles(p, 0, ALL[RING:])
                else:
                    head = NB if first_visit(p) else RING
                    tiles(p, 0, ALL[:head])
                    if 1 <= p < PASSES:
                        spread_den(p - 1)
                    if p > PASSES:
                        sp.wait_ge(s["agg_done"], p - 1)
                        load_rec(p - 1)
                    next_f1(p)
                    tiles(p, 0, ALL[head:CYCLE - 2])
                    if 1 <= p < PASSES:
                        spread_rec(p - 1)
                    tiles(p, 0, ALL[CYCLE - 2:])
                with sp.Fori(1, ITS - 1) as it:
                    tiles(p, it)
                tiles(p, ITS - 1)
            sp.wait_ge(s["agg_done"], 2 * PASSES - 1)
            load_rec(2 * PASSES - 1)

            sp.wait_ge(s["e_used"], halves(2 * PASSES * NT))
            sp.dma_start(xn, x.rearrange("(t p) f -> p t f", p=P)).then_inc(s["xn_in"], 16)

            sp.wait_ge(s["agg_done"], 2 * PASSES)
            adj_v = adj8.rearrange("(t p) n -> p t n", p=P)

            def load_group(g, slot):
                sp.dma_start(adjg_w[:, slot, :, :], adj_v[:, :, ds(g * (GI // 4), GI // 4)]).then_inc(adjg_in[slot], 16)

            def store_group(g):
                for k in range(GT):
                    sp.wait_ge(s["y_ready"], GT * g + k + 1)
                    sp.dma_start(out[ds(g * GI + k * P, P), :], ybuf[:, k, :]).then_inc(out_free[k], 16)

            load_group(0, 0)
            load_group(1, 1)
            with sp.Fori(0, NG // 2 - 1) as gg:
                for v in range(2):
                    sp.wait_ge(s["u_full"], GT * (2 * gg + v + 1))
                    load_group(2 * gg + v + 2, v)
                    store_group(2 * gg + v)
            for g in range(NG - 2, NG):
                store_group(g)
            for k in range(GT):
                sp.wait_ge(out_free[k], 16 * NG + 16)

        @block.gpsimd
        def _(pool):
            pool.memset(wm[:, :, :], 0.0).then_inc(s["zeroed"], 1)
            pool.memset(wtbd[:, :, :], 0.0).then_inc(s["zeroed"], 1)
            pool.memset(vbd[:, :, :], 0.0).then_inc(s["zeroed"], 1)
            pool.memset(ident[:, :], 0.0).then_inc(s["ident_set"], 1)
            pool.wait_ge(s["ident_set"], 1)
            pool.affine_select(out=ident[:, :], in_=ident[:, :], compare_op=ALU.not_equal, fill=1.0,
                               base=0, pattern=[[-1, P]], channel_multiplier=1).then_inc(s["ident_set"], 1)
            pool.memset(vx[:, :, :, :], 1.0).then_inc(s["ones_set"], 1)
            pool.memset(ones16[:, :], 1.0).then_inc(s["ones_set"], 1)
            pool.memset(eps[:, 0:1], EPS_BN).then_inc(s["ones_set"], 1)
            pool.memset(eps[:, 1:2], EPS_LN).then_inc(s["ones_set"], 1)
            pool.wait_ge(s["ones_set"], 4)

            def steps(p, it):
                for u in ALL:
                    n = tile_of(it, u)
                    if not very_first(p, it, u):
                        pool.wait_ge(s["e_used"], halves(NT * p + n - RING + 1))
                    v = vals[:, ds(n, 1), pair(p) * P:(pair(p) + 1) * P].rearrange("p a c -> p (a c)")
                    w, w16 = vx[:, u % RING, :, :], vx16[:, u % RING, :]
                    if p < PASSES:
                        pool.tensor_copy(w[:, :, 0:D], v.rearrange("p (h d) -> p h d", h=HP))\
                            .then_inc(s["vx_ready"], 1)
                    elif u in KEPT + SPLIT:
                        two = sorted(KEPT + SPLIT)
                        k = len(two) * (ITS * (p - PASSES) + it) + two.index(u)
                        his = (w16[:, 0:D], w16[:, 3 * D:4 * D])
                        for h in range(HP):
                            pool.tensor_copy(his[h], v[:, h * D:(h + 1) * D]).then_inc(s["v_step"], 1)
                        pool.wait_ge(s["v_step"], 4 * k + 2)
                        held(pool)
                        for h in range(HP):
                            pool.tensor_tensor(vd[:, h * D:(h + 1) * D], v[:, h * D:(h + 1) * D], his[h],
                                               ALU.subtract).then_inc(s["v_step"], 1)
                        pool.wait_ge(s["v_step"], 4 * k + 4)
                        held(pool)
                        pool.tensor_scalar(w16[:, D:3 * D], vd[:, :], SCALE, None, ALU.mult)\
                            .then_inc(s["vx_ready"], 1)
                    else:
                        pool.tensor_copy(w[:, 0, 0:D], v[:, 0:D])
                        pool.tensor_copy(w[:, 1, D:P], v[:, D:P]).then_inc(s["vx_ready"], 1)

            for p in range(2 * PASSES):
                if p == 0:
                    pool.wait_ge(s["xw_free"], NT)
                if p == PASSES:
                    pool.wait_ge(s["e_used"], halves(NT * PASSES))
                    pool.memset(vx[:, :, :, :], 0.0).then_inc(s["vx_zero"], 1)
                    pool.wait_ge(s["vx_zero"], 1)
                    pool.wait_ge(s["tr_copied"], NT // 2)
                steps(p, 0)
                with pool.Fori(1, ITS) as it:
                    steps(p, it)

        @block.scalar
        def _(act):
            def slot_free(p, it, u, h):
                if very_first(p, it, u):
                    if u < 2:
                        act.wait_ge(s["xw_free"], u + 1)
                    else:
                        act.wait_ge(s["xw_free"], NT)
                        act.wait_ge(s["f1_copied"], NC)
                    return
                q, jt, v = before(p, it, u)
                if q >= PASSES and v in SPLIT:
                    act.wait_ge(s["split_done"], halves(splits(q, jt, v), h))
                    return
                if q >= PASSES and v in KEPT:
                    h = HP - 1
                act.wait_ge(s["e_used"], halves(NT * q + tile_of(jt, v) + 1, h))
                if q < PASSES and v in KEPT:
                    act.wait_ge(s["lo_split"], kept(q, jt, v))

            def steps(p, it, us=ALL):
                for u in us:
                    if u in computed(p):
                        for h in range(HP):
                            k = pair(p) * HP + h
                            slot_free(p, it, u, h)
                            act.activation(ering[:, u % RING, h * CH:(h + 1) * CH], f1b[:, p % 2, h, :], ACT.Tanh,
                                           bias=f2h[:, ds(tile_of(it, u), 1), k], scale=0.5)\
                                .then_inc(s["tanh_done"], 1)
                        for h in range(HP):
                            e = ering[:, u % RING, h * CH:(h + 1) * CH]
                            act.wait_ge(s["tanh_done"], halves(made(p, it, u), h))
                            act.activation(e, e, ACT.Exp, scale=0.5).then_inc(s["e_ready"], 1)

            def elu_parts(k, v, full, free, room, bank, tmp, slot, bias):
                act.wait_ge(s[full], k + 1)
                if isinstance(k, int) and k == 0:
                    for stored in ("hi_stored", "lo_stored"):
                        act.wait_ge(s[stored], 16 * kept(PASSES - 1, ITS - 1, KEPT[-1]))
                if not (isinstance(k, int) and k < 4):
                    act.wait_ge(s[room], k - 3)
                b = cols[:, v % 2, bias:bias + 1] if bias is not None else 0.0
                act.activation(tmp[:, 0, slot + v, :], ps[:, bank + v, :], ACT.Exp, bias=b)
                act.activation(tmp[:, 1, slot + v, :], ps[:, bank + v, :], ACT.Relu, bias=b).then_inc(s[free], 1)

            def bn_sqrt(k):
                act.wait_ge(s["bn_mv"], k + 1)
                act.activation(bnc[:, k, :, 0], mv[:, :, 1], ACT.Sqrt, bias=eps[:, 0:1]).then_inc(s["bn_sd"], 1)

            def encoder():
                def piece(c, v):
                    for o in range(NB):
                        elu_parts(2 * c + o, 2 * v + o, "z_full", "z_free", "h_ready", 0, tmp_enc, 0, 2)

                for c in range(2):
                    piece(c, c)
                with act.Fori(1, NC // 2) as i:
                    for v in range(2):
                        piece(2 * i + v, v)
                bn_sqrt(1)
                with act.Fori(0, 2) as i:
                    for v in range(NC):
                        act.wait_ge(s["tr_full"], NC * i + v + 1)
                        act.activation(vals[:, ds(2 * (NC * i + v), 2), :].rearrange("p a f -> p (a f)"),
                                       ps[:, v, :], ACT.Copy).then_inc(s["tr_copied"], 1)

            def decoder():
                def y_piece(c, v):
                    for o in range(NB):
                        elu_parts(2 * c + o, 2 * v + o, "y_full", "y_free", "yc_ready", 4, tmp_dec, 4, None)

                def z_piece(c, v):
                    for o in range(NB):
                        elu_parts(2 * NC + 2 * c + o, 2 * v + o, "z_full", "z_free", "h_ready", 0, tmp_dec, 0, 5)

                y_piece(0, 0)
                for c in range(2):
                    y_piece(c + 1, (c + 1) % 2)
                    z_piece(c, c)
                with act.Fori(1, NC // 2 - 1) as i:
                    for v in range(2):
                        y_piece(2 * i + v + 1, (v + 1) % 2)
                        z_piece(2 * i + v, v)
                y_piece(NC - 1, 1)
                z_piece(NC - 2, 0)
                z_piece(NC - 1, 1)

            def affine_out(c):
                for b in range(NB):
                    a = agg[:, b, c * BK:(c + 1) * BK]
                    act.activation(a, a, ACT.Identity, scale=bnc[:, 2, b, 1:2], bias=bnc[:, 2, b, 3:4])\
                        .then_inc(s["emb_ready"], 1)

            def ln_sqrt(g):
                act.wait_ge(s["ln_aggr"], 8 * (g + 1))
                act.activation(lnsd[:, 8 * g:8 * g + 8, 0], lnmv[:, 8 * g:8 * g + 8, 1], ACT.Sqrt,
                               bias=eps[:, 1:2]).then_inc(s["ln_sd"], 1)

            def hi(g):
                act.wait_ge(s["x1_done"], 8 * (g + 1))
                act.activation(x1s[:, 8 * g:8 * g + 8, 0:F], vals[:, 8 * g:8 * g + 8, :], ACT.Copy)\
                    .then_inc(s["hi_made"], 1)

            def lo(g):
                act.wait_ge(s["d_made"], g + 1)
                act.activation(x1s[:, 8 * g:8 * g + 8, F:2 * F], dtmp[:, 8 * (g % 2):8 * (g % 2) + 8, :],
                               ACT.Copy, scale=SCALE).then_inc(s["lo_made"], 1)

            act.wait_ge(s["ones_set"], 4)
            for p in range(2 * PASSES):
                act.wait_ge(f1_in[p % 2], 32 * (p // 2 + 1))
                steps(p, 0, ALL[:RING])
                if p == PASSES:
                    act.wait_ge(s["cols_in"], 16 * 8)
                    bn_sqrt(0)
                    encoder()
                steps(p, 0, ALL[RING:])
                with act.Fori(1, ITS) as it:
                    steps(p, it)
            decoder()
            bn_sqrt(2)
            act.wait_ge(s["bn_step"], 4 * 3)
            for c in range(4):
                affine_out(c)
            ln_sqrt(0)
            affine_out(4)
            affine_out(5)
            ln_sqrt(1)
            hi(0)
            affine_out(6)
            affine_out(7)
            ln_sqrt(2)
            hi(1)
            lo(0)
            ln_sqrt(3)
            hi(2)
            lo(1)
            hi(3)
            lo(2)
            lo(3)

            with act.Fori(0, NG // 2) as gg:
                for v in range(2):
                    g = 2 * gg + v
                    for k in range(GT):
                        act.wait_ge(s["u_full"], GT * g + k + 1)
                        act.activation(utmp[:, k, :], ps[:, k, F:2 * F], ACT.Copy, scale=1.0 / SCALE)\
                            .then_inc(s["lo_scaled"], 1)
                        if k == 0:
                            act.wait_ge(s["deg_full"], g + 1)
                            act.activation(degs[:, 0, :], deg_psum(v), ACT.Sqrt).then_inc(s["deg_sqrt"], 1)
                        act.wait_ge(s["y_step"], 3 * (GT * g + k) + 3)
                        act.activation(degs[:, 7, k:k + 1], lnmv[:, k, 1:2], ACT.Sqrt, bias=eps[:, 1:2])\
                            .then_inc(s["y_sqrt"], 1)

        @block.vector
        def _(dve):
            dve.wait_ge(s["wv_done"], 1)
            dve.tensor_copy(wm[:, :, P:P + 2 * H],
                            ps[:, 0, 0:NB * 2 * H].rearrange("p (b c) -> p b c", b=NB)).then_inc(s["wv_copied"], 1)
            def f1_rows(c):
                for u in range(4):
                    dve.wait_ge(s["f1_full"], 4 * c + u + 1)
                    dve.tensor_copy(agg[0:H, 0, (4 * c + u) * BK:(4 * c + u + 1) * BK], ps[0:H, u, :])\
                        .then_inc(s["f1_copied"], 1)

            f1_rows(0)
            with dve.Fori(0, NT // RING) as it:
                for u in range(RING):
                    n = it * RING + u
                    bank = ps[:, 4 + u, 0:NB * (P + 2 * H)].rearrange("p (b c) -> p b c", b=NB)
                    dve.wait_ge(s["xw_full"], n + 1)
                    dve.tensor_copy(vals[:, ds(n, 1), :].rearrange("p a (b c) -> p (a b) c", b=NB), bank[:, :, 0:P])
                    for b in range(NB):
                        last = dve.tensor_scalar(f2h[:, ds(n, 1), b * HP:(b + 1) * HP],
                                                 bank[:, b:b + 1, P + H + b * HP:P + H + (b + 1) * HP],
                                                 0.5, None, ALU.mult)
                    last.then_inc(s["xw_free"], 1)
            f1_rows(1)

            def masks(p, it, us=ALL):
                for u in us:
                    if u not in computed(p):
                        continue
                    n = tile_of(it, u)
                    slot = u % RING
                    if first_visit(p):
                        dve.wait_ge(stage_in[u % 2], 16 * (visit(p) * NT // 2 + it * CYCLE // 2 + u // 2 + 1))
                        if not very_first(p, it, u):
                            dve.wait_ge(adj_stored[slot], 16 * (visit(p) * NT // RING + it * CYCLE // RING + u // RING))
                        held(dve)
                        dve.tensor_copy(mask[:, slot, :], stage[:, u % 2, :], saturate=False)\
                            .then_inc(s["mask_conv"], 1)
                        dve.wait_ge(s["mask_conv"], visit(p) * NT + n + 1)
                    else:
                        dve.wait_ge(mask_in[slot], 16 * loads(p, it, u))
                    for h in range(HP):
                        e = ering[:, slot, h * CH:(h + 1) * CH]
                        dve.wait_ge(s["e_ready"], halves(made(p, it, u), h))
                        held(dve)
                        if p < PASSES:
                            dve.tensor_tensor(e, e, mask[:, slot, :], ALU.mult).then_inc(s["p_ready"], 1)
                        else:
                            dve.scalar_tensor_tensor(out=e, in0=e, scalar=SCALE, in1=mask[:, slot, :],
                                                     op0=ALU.mult, op1=ALU.mult).then_inc(s["p_ready"], 1)
                    if p < PASSES and u in KEPT:
                        keep(p, it, u)
                    if p >= PASSES and u in SPLIT and not (p == PASSES and first_it(it) and u < RING):
                        split(p, it, u)

            def keep(p, it, u):
                k = kept(p, it, u)
                hi, lo = hi_lo(p)
                e = ering[:, u % RING, :]
                first = p == 0 and first_it(it) and u == KEPT[0]
                if first:
                    dve.wait_ge(s["f1_copied"], NC)
                    dve.wait_ge(s["f1_stored"], 32)
                else:
                    dve.wait_ge(s["hi_stored"], 16 * (k - 1))
                dve.wait_ge(s["p_ready"], halves(made(p, it, u)))
                dve.tensor_scalar(hi, e, SCALE, None, ALU.mult).then_inc(s["hi_split"], 1)
                if not first:
                    dve.wait_ge(s["lo_stored"], 16 * (k - 1))
                dve.wait_ge(s["hi_split"], k)
                dve.scalar_tensor_tensor(out=lo, in0=e, scalar=SCALE, in1=hi,
                                         op0=ALU.mult, op1=ALU.subtract).then_inc(s["lo_split"], 1)

            def split(p, it, u):
                k = splits(p, it, u)
                parts = [(ering[:, u % RING, h * CH:(h + 1) * CH], split16[:, h * CH:(h + 1) * CH],
                          split16[:, (HP + h) * CH:(HP + h + 1) * CH]) for h in range(HP)]
                q, jt, v = before(p, it, u, lambda q, u: SPLIT)
                for h, (e, hi, lo) in enumerate(parts):
                    dve.wait_ge(s["p_ready"], halves(made(p, it, u), h))
                    if q >= PASSES:
                        dve.wait_ge(s["e_used"], halves(NT * q + tile_of(jt, v) + 1, h))
                    dve.tensor_copy(hi, e).then_inc(s["split_step"], 1)
                for h, (e, hi, lo) in enumerate(parts):
                    dve.wait_ge(s["split_step"], halves(k, h))
                    dve.tensor_tensor(lo, e, hi, ALU.subtract).then_inc(s["split_done"], 1)

            def evacuate(p):
                if p == PASSES - 2:
                    for stored in ("hi_stored", "lo_stored"):
                        dve.wait_ge(s[stored], 16 * kept(p, ITS - 1, KEPT[-1]))
                for h in range(HP):
                    dve.wait_ge(s["e_used"], halves(NT * (p + 1), h))
                    rows = slice(D * h, D * h + D)
                    a = agg[rows, pair(p), chunk(p) * CH:(chunk(p) + 1) * CH].rearrange("p (k n) -> p k n", k=4)
                    banks = slice(4 * h, 4 * h + 4)
                    if p < PASSES:
                        dve.tensor_copy(a, ps[0:D, banks, :]).then_inc(s["evacuated"], 1)
                        dve.tensor_copy(rden[D * h:D * h + 1, :].rearrange("p (k n) -> p k n", k=4),
                                        ps[D:D + 1, banks, :]).then_inc(s["evacuated"], 1)
                    else:
                        k = HP * (p - PASSES) + h + 1
                        dve.tensor_scalar(a, ps[D * (1 - h):D * (1 - h) + D, banks, :], 1.0 / SCALE, None, ALU.mult)\
                            .then_inc(s["u_step"], 1)
                        dve.wait_ge(s["u_step"], k)
                        dve.tensor_tensor(a, ps[rows, banks, :], a, ALU.add).then_inc(s["evacuated"], 1)

            def reciprocals(p):
                dve.wait_ge(s["den_in"], 32 * (p + 1))
                dve.tensor_scalar(dsm[:, :], dsm[:, :], TINY, None, ALU.max).then_inc(s["rec_made"], 1)
                dve.wait_ge(s["rec_made"], 2 * p + 1)
                dve.reciprocal(rsm[:, :], dsm[:, :]).then_inc(s["rec_made"], 1)

            def normalise(p):
                dve.wait_ge(s["rden_in"], 32 * (p + 1))
                dve.wait_ge(s["evacuated"], evacuations(p))
                a = agg[:, pair(p), chunk(p) * CH:(chunk(p) + 1) * CH]
                if p < PASSES:
                    dve.tensor_tensor(a, a, rden[:, :], ALU.mult).then_inc(s["agg_done"], 1)
                    dve.wait_ge(s["agg_done"], p + 1)
                    for k in range(4):
                        c = chunk(p) * 4 + k
                        last = dve.bn_stats(stats[:, pair(p), c, :], agg[:, pair(p), c * BK:(c + 1) * BK])
                    return last
                dve.scalar_tensor_tensor(out=a, in0=a, scalar=1.0 / SCALE, in1=rden[:, :], op0=ALU.mult,
                                         op1=ALU.mult).then_inc(s["agg_done"], 1)

            step = [0]

            def link(ins):
                step[0] += 1
                ins.then_inc(s["bn_step"], 1)
                dve.wait_ge(s["bn_step"], step[0])

            def bn_coefficients(k, gamma, beta):
                for b in range(NB):
                    last = dve.bn_aggr(mv[:, b, :], stats[:, b, :, :].rearrange("p c s -> p (c s)"))
                last.then_inc(s["bn_mv"], 1)
                dve.wait_ge(s["bn_mv"], k + 1)
                dve.wait_ge(s["bn_sd"], k + 1)
                c = bnc[:, k, :, :]
                link(dve.reciprocal(c[:, :, 1], c[:, :, 0]))
                link(dve.tensor_tensor(c[:, :, 1], c[:, :, 1], cols[:, :, gamma], ALU.mult))
                link(dve.tensor_tensor(c[:, :, 2], mv[:, :, 0], c[:, :, 1], ALU.mult))
                link(dve.tensor_tensor(c[:, :, 3], cols[:, :, beta], c[:, :, 2], ALU.subtract))

            def h_piece(base, c, v, tmp, src, dst):
                k = base + 2 * c
                cc = ds(c * BK, BK)
                for o in range(NB):
                    e, r = tmp[:, 0, 2 * v + o, :], tmp[:, 1, 2 * v + o, :]
                    dve.wait_ge(s["z_free"], k + o + 1)
                    dve.scalar_tensor_tensor(out=r, in0=e, scalar=1.0, in1=r, op0=ALU.min, op1=ALU.add)\
                        .then_inc(s["elu_step"], 1)
                dve.wait_ge(s["z_full"], k + 2)
                for o in range(NB):
                    dve.wait_ge(s["elu_step"], 2 * k + o + 1)
                    dve.scalar_tensor_tensor(out=dst[:, o, cc], in0=tmp[:, 1, 2 * v + o, :], scalar=-1.0,
                                             in1=src[:, o, cc], op0=ALU.add, op1=ALU.add)\
                        .then_inc(s["elu_step"], 1)
                for o in range(NB):
                    dve.wait_ge(s["elu_step"], 2 * k + NB + o + 1)
                    dve.bn_stats(stats[:, o, ds(c, 1), :], dst[:, o, cc]).then_inc(s["h_ready"], 1)

            def yc_piece(c, v):
                k = 2 * c
                for o in range(NB):
                    e, r = tmp_dec[:, 0, 4 + 2 * v + o, :], tmp_dec[:, 1, 4 + 2 * v + o, :]
                    dve.wait_ge(s["y_free"], k + o + 1)
                    dve.scalar_tensor_tensor(out=r, in0=e, scalar=1.0, in1=r, op0=ALU.min, op1=ALU.add)\
                        .then_inc(s["y_step0"], 1)
                for o in range(NB):
                    dve.wait_ge(s["y_step0"], k + o + 1)
                    dve.tensor_scalar(yc[:, o, ds(c * BK, BK)], tmp_dec[:, 1, 4 + 2 * v + o, :], -1.0, None,
                                      ALU.add).then_inc(s["yc_ready"], 1)

            def encoder():
                bn_coefficients(0, 0, 1)
                for cc in (slice(0, BK), slice(BK, N)):
                    for b in range(NB):
                        dve.tensor_scalar(agg[:, b, cc], agg[:, b, cc], bnc[:, 0, b, 1:2], bnc[:, 0, b, 3:4],
                                          ALU.mult, ALU.add).then_inc(s["xn_ready"], 1)
                dve.wait_ge(s["xn_ready"], 2 * NB)
                with dve.Fori(0, NC // 2) as i:
                    for v in range(2):
                        h_piece(0, 2 * i + v, v, tmp_enc, agg, agg)
                dve.wait_ge(s["h_ready"], 2 * NC)
                bn_coefficients(1, 3, 4)
                for c in range(NC):
                    for b in range(NB):
                        a = agg[:, b, c * BK:(c + 1) * BK]
                        dve.tensor_scalar(a, a, bnc[:, 1, b, 1:2], bnc[:, 1, b, 3:4], ALU.mult, ALU.add)\
                            .then_inc(s["em_ready"], 1)

            for p in range(2 * PASSES):
                if p == PASSES:
                    evacuate(p - 1)
                    masks(p, 0, (0, 1))
                    reciprocals(p - 1)
                    masks(p, 0, (2, 3))
                    normalise(p - 1).then_inc(s["stats_done"], 1)
                    dve.wait_ge(s["stats_done"], 1)
                    dve.wait_ge(s["cols_in"], 16 * 8)
                    encoder()
                    for u in SPLIT:
                        if u < RING:
                            split(p, 0, u)
                else:
                    masks(p, 0, (0,))
                    if p:
                        evacuate(p - 1)
                    masks(p, 0, (1, 2, 3))
                masks(p, 0, (4,))
                if 1 <= p < PASSES:
                    reciprocals(p - 1)
                masks(p, 0, (5, 6, 7))
                masks(p, 1)
                if p >= 1 and p != PASSES:
                    normalise(p - 1)
                with dve.Fori(2, ITS) as it:
                    masks(p, it)
            evacuate(2 * PASSES - 1)
            normalise(2 * PASSES - 1)

            yc_piece(0, 0)
            with dve.Fori(0, NC // 2 - 1) as i:
                for v in range(2):
                    yc_piece(2 * i + v + 1, (v + 1) % 2)
                    h_piece(2 * NC, 2 * i + v, v, tmp_dec, yc, agg)
            yc_piece(NC - 1, 1)
            h_piece(2 * NC, NC - 2, 0, tmp_dec, yc, agg)
            h_piece(2 * NC, NC - 1, 1, tmp_dec, yc, agg)
            dve.wait_ge(s["h_ready"], 4 * NC)
            bn_coefficients(2, 6, 7)

            def sums(g):
                def tile_stats(j):
                    dve.wait_ge(s["sum_ready"], j + 1)
                    for t in range(2 * j, 2 * j + 2):
                        last = dve.bn_stats(lnst[:, t, :], vals[:, t, :])
                    return last

                for j in range(4 * g, 4 * g + 4):
                    dve.wait_ge(s["tr_full"], NT // 2 + j + 1)
                    dve.tensor_tensor(vals[:, 2 * j:2 * j + 2, :].rearrange("p a f -> p (a f)"), ps[:, j % 8, :],
                                      xn[:, 2 * j:2 * j + 2, :].rearrange("p a f -> p (a f)"), ALU.add)\
                        .then_inc(s["sum_ready"], 1)
                    if j > 4 * g:
                        tile_stats(j - 1)
                link(tile_stats(4 * g + 3))
                for t in range(8 * g, 8 * g + 8):
                    dve.bn_aggr(lnmv[:, t, :], lnst[:, t, :]).then_inc(s["ln_aggr"], 1)

            def norm(g):
                dve.wait_ge(s["ln_sd"], g + 1)
                t8 = slice(8 * g, 8 * g + 8)
                dve.reciprocal(lnsd[:, t8, 1], lnsd[:, t8, 0]).then_inc(s["ln_rec"], 1)
                dve.wait_ge(s["ln_rec"], g + 1)
                dve.wait_ge(s["ln_aggr"], 8 * (g + 1))
                for t in range(8 * g, 8 * g + 8):
                    dve.tensor_scalar(vals[:, t, :], vals[:, t, :], lnmv[:, t, 0:1], lnsd[:, t, 1:2],
                                      ALU.subtract, ALU.mult).then_inc(s["x1_done"], 1)

            def rest(g):
                t8 = slice(8 * g, 8 * g + 8)
                dve.wait_ge(s["hi_made"], g + 1)
                if g >= 2:
                    dve.wait_ge(s["lo_made"], g - 1)
                dve.tensor_tensor(dtmp[:, 8 * (g % 2):8 * (g % 2) + 8, :], vals[:, t8, :], x1s[:, t8, 0:F],
                                  ALU.subtract).then_inc(s["d_made"], 1)

            dve.wait_ge(s["xn_in"], 16)
            sums(0)
            sums(1)
            norm(0)
            sums(2)
            norm(1)
            rest(0)
            sums(3)
            dve.memset(degs[:, :, :], 0.0).then_inc(s["u_free"], GT)
            norm(2)
            rest(1)
            norm(3)
            rest(2)
            rest(3)

            for k in range(GT):
                dve.memset(ybuf[:, k, 0:1], 0.0).then_inc(out_free[k], 16)
            def fold(gg, v, k):
                n = GT * (2 * gg + v - 2) + k
                cc = slice(k * P, (k + 1) * P)
                if k == 0:
                    dve.wait_ge(adjg_in[v], 16 * (gg + 1))
                    held(dve)
                dve.tensor_tensor(fold1[:, :, cc], adjg[:, v, 0:NT // 2, cc], adjg[:, v, NT // 2:NT, cc], ALU.add,
                                  saturate=False)\
                    .then_inc(s["fold_step"], 1)
                dve.wait_ge(s["fold_step"], n + 1)
                held(dve)
                dve.tensor_tensor(fold2[:, v, :, cc], fold1[:, 0:NT // 4, cc], fold1[:, NT // 4:NT // 2, cc], ALU.add,
                                  saturate=False)\
                    .then_inc(s["folded"], 1)

            def degrees(g, v):
                def step(i, ins):
                    ins.then_inc(s["deg_step"], 1)
                    dve.wait_ge(s["deg_step"], 7 * g + i + 1)

                d = [degs[:, i, :] for i in range(8)]
                dve.wait_ge(s["deg_sqrt"], g + 1)
                step(0, dve.tensor_copy(d[1], deg_psum(v)))
                step(1, dve.tensor_scalar(d[2], d[0], EPS_NORM, None, ALU.max))
                step(2, dve.reciprocal(d[3], d[2]))
                step(3, dve.tensor_scalar(d[4], d[3], 1.0, None, ALU.add))
                step(4, dve.tensor_tensor(d[5], d[4], d[1], ALU.mult))
                step(5, dve.reciprocal(d[6], d[5]))
                step(6, dve.tensor_tensor(d[6], d[6], d[4], ALU.mult))

            def row_tile(g, v, k):
                r = GT * g + k
                dve.wait_ge(s["lo_scaled"], r + 1)
                dve.tensor_tensor(utmp[:, k, :], ps[:, k, 0:F], utmp[:, k, :], ALU.add).then_inc(s["u_free"], 1)
                if k == 0:
                    degrees(g, v)
                dve.wait_ge(s["u_free"], GT + r + 1)
                dve.scalar_tensor_tensor(out=utmp[:, k, :], in0=utmp[:, k, :], scalar=degs[:, 6, k:k + 1],
                                         in1=vals[:, ds(r, 1), :].rearrange("p a f -> p (a f)"),
                                         op0=ALU.mult, op1=ALU.add).then_inc(s["y_step"], 1)
                dve.wait_ge(s["y_step"], 3 * r + 1)
                dve.bn_stats(lnst[:, k, :], utmp[:, k, :]).then_inc(s["y_step"], 1)
                dve.wait_ge(s["y_step"], 3 * r + 2)
                held(dve)
                dve.bn_aggr(lnmv[:, k, :], lnst[:, k, :]).then_inc(s["y_step"], 1)
                dve.wait_ge(s["y_sqrt"], r + 1)
                dve.reciprocal(lnsd[:, k, 1:2], degs[:, 7, k:k + 1]).then_inc(s["fin_step"], 1)
                dve.wait_ge(s["fin_step"], r + 1)
                dve.wait_ge(out_free[k], 16 * g + 16)
                dve.tensor_scalar(ybuf[:, k, :], utmp[:, k, :], lnmv[:, k, 0:1], lnsd[:, k, 1:2],
                                  ALU.subtract, ALU.mult).then_inc(s["y_ready"], 1)

            for k in range(GT):
                row_tile(0, 0, k)
            for k in range(GT):
                fold(1, 0, k)
                row_tile(1, 1, k)
            with dve.Fori(1, NG // 2 - 1) as gg:
                for v in range(2):
                    for k in range(GT):
                        fold(gg + v, 1 - v, k)
                        row_tile(2 * gg + v, v, k)
            for k in range(GT):
                fold(NG // 2 - 1, 1, k)
                row_tile(NG - 2, 0, k)
            for k in range(GT):
                row_tile(NG - 1, 1, k)

        @block.tensor
        def _(pe):
            pe.wait_ge(s["wt_in"], 16 * 2 * H)
            for b in range(NB):
                last = pe.matmul(ps[:, 0, b * 2 * H:(b + 1) * 2 * H], wtbd[:, b, :], vbd[:, b, :],
                                 start=True, stop=True)
            last.then_inc(s["wv_done"], 1)
            pe.wait_ge(s["wv_copied"], 1)


            def f1_rows(c):
                if c >= 4:
                    pe.wait_ge(s["f1_copied"], c - 3)
                if c % 2 == 0:
                    pe.wait_ge(x_in[c // 2], 16)
                for b in range(NB):
                    last = pe.matmul(ps[0:H, c % 4, :], wm[:, b, P:P + H], xTs[:, b, c * BK:(c + 1) * BK],
                                     start=(b == 0), stop=(b == NB - 1))
                last.then_inc(s["f1_full"], 1)

            for c in range(4):
                f1_rows(c)
            pe.wait_ge(s["w_in"], 16 * H)
            for n in range(NT):
                if n >= RING:
                    pe.wait_ge(s["xw_free"], n - RING + 1)
                if n % 8 == 0:
                    pe.wait_ge(x_in[n // 8], 16)
                for b in range(NB):
                    last = pe.matmul(ps[:, 4 + n % RING, b * (P + 2 * H):(b + 1) * (P + 2 * H)],
                                     xTs[:, b, n * P:(n + 1) * P], wm[:, b, :], start=True, stop=True)
                last.then_inc(s["xw_full"], 1)
            for c in range(4, NC):
                f1_rows(c)
            pe.wait_ge(s["xw_free"], NT)
            pe.wait_ge(s["f1_copied"], NC)

            def steps(p, it):
                for u in ALL:
                    slot = u % RING
                    fixed = isinstance(it, int)
                    start, stop = fixed and it == 0 and u == 0, fixed and it == ITS - 1 and u == CYCLE - 1
                    pe.wait_ge(s["vx_ready"], NT * p + tile_of(it, u) + 1)
                    if u not in computed(p):
                        pe.wait_ge(e_loaded[slot], 16 * loaded(p, it, u))
                    for h in range(HP):
                        if p >= PASSES and u in SPLIT:
                            pe.wait_ge(s["split_done"], halves(splits(p, it, u), h))
                        elif u in computed(p):
                            pe.wait_ge(s["p_ready"], halves(made(p, it, u), h))
                        if start and p % PASSES:
                            before_it = evacuations(p - 1) - evacuations(p - 2) if p > 1 else 4
                            pe.wait_ge(s["evacuated"], evacuations(p - 1) - (HP - 1 - h) * before_it // HP)
                        for c in range(4):
                            bank = ps[:, 4 * h + c, :]
                            at = h * CH + c * BK
                            if p < PASSES:
                                last = pe.matmul(bank[0:D + 1, :], vx[:, slot, h, 0:D + 1], ering[:, slot, at:at + BK],
                                                 start=start, stop=stop)
                            elif u not in KEPT + SPLIT:
                                last = pe.matmul(bank, vx[:, slot, h, :], ering[:, slot, at:at + BK],
                                                 start=start, stop=stop)
                            else:
                                parts = ering16[:, slot, :] if u in KEPT else split16
                                for a in range(2):
                                    last = pe.matmul(bank, vx16[:, slot, h * P:(h + 1) * P],
                                                     parts[:, a * HP * CH + at:a * HP * CH + at + BK],
                                                     start=start and a == 0, stop=stop and a == 1)
                        last.then_inc(s["e_used"], 1)

            def z_chunk(w, src, c, base):
                for o in range(NB):
                    k = base + 2 * c + o
                    if k >= 4:
                        pe.wait_ge(s["z_free"], k - 3)
                    for b in range(NB):
                        last = pe.matmul(ps[:, k % 4, :], w[:, b, o * P:(o + 1) * P],
                                         src[:, b, c * BK:(c + 1) * BK], start=(b == 0), stop=(b == NB - 1))
                    last.then_inc(s["z_full"], 1)

            def transposes(c, bank):
                for q in range(2):
                    for t in range(2):
                        for b in range(NB):
                            n = 4 * c + 2 * q + t
                            last = pe.transpose(ps[:, bank + q, t * F + b * P:t * F + (b + 1) * P],
                                                agg[:, b, n * P:(n + 1) * P], ident[:, :])
                    last.then_inc(s["tr_full"], 1)

            for p in range(2 * PASSES):
                if p == PASSES:
                    pe.wait_ge(s["mlp_in"], 32)
                    pe.wait_ge(s["ident_set"], 2)
                    pe.wait_ge(s["evacuated"], evacuations(p - 1))
                    for c in range(NC):
                        pe.wait_ge(s["xn_ready"], NB if c == 0 else 2 * NB)
                        z_chunk(wenc, agg, c, 0)
                    pe.wait_ge(s["z_free"], 2 * NC)
                    for c in range(NC):
                        pe.wait_ge(s["em_ready"], 2 * c + 2)
                        if c >= 4:
                            pe.wait_ge(s["tr_copied"], 2 * (c - 3))
                        transposes(c, 2 * (c % 4))
                    pe.wait_ge(s["tr_copied"], 2 * NC)
                steps(p, 0)
                with pe.Fori(1, ITS - 1) as it:
                    steps(p, it)
                steps(p, ITS - 1)

            def y_chunk(c):
                pe.wait_ge(s["agg_done"], 2 * PASSES if c >= NC // NCH else 2 * PASSES - NB)
                for o in range(NB):
                    k = 2 * c + o
                    if k >= 4:
                        pe.wait_ge(s["y_free"], k - 3)
                    pe.matmul(ps[:, 4 + k % 4, :], wtbd[:, o, :], agg[:, o, c * BK:(c + 1) * BK],
                              start=True, stop=True).then_inc(s["y_full"], 1)

            pe.wait_ge(s["evacuated"], evacuations(2 * PASSES - 1))
            y_chunk(0)
            y_chunk(1)
            for c in range(NC):
                pe.wait_ge(s["yc_ready"], 2 * c + 2)
                z_chunk(wdec, yc, c, 2 * NC)
                if c + 2 < NC:
                    y_chunk(c + 2)
            pe.wait_ge(s["z_free"], 4 * NC)
            pe.wait_ge(s["y_free"], 2 * NC)
            for c in range(NC):
                pe.wait_ge(s["emb_ready"], 2 * c + 2)
                if c >= 4:
                    pe.wait_ge(s["sum_ready"], 2 * (c - 3))
                transposes(c, 2 * (c % 4))

            def row_tile(v, k, tiles):
                for t in tiles:
                    last = pe.matmul(ps[:, k, :], adjg[:, v, t, k * P:(k + 1) * P], x1s[:, t, :],
                                     start=(t == 0), stop=(t == NT - 1))
                return last

            def degrees(v, g):
                if not isinstance(g, int):
                    pe.wait_ge(s["folded"], GT * (g - 1))
                    held(pe)
                src = adjg[:, v, :, :] if isinstance(g, int) else fold2[:, v, :, :]
                nt = NT if isinstance(g, int) else NT // 4
                for k in range(GT):
                    for t in range(nt):
                        last = pe.matmul(ps[:, 4 + v, 2 * k:2 * k + 2], src[:, t, k * P:(k + 1) * P],
                                         ones16[:, :], start=(t == 0), stop=(t == nt - 1))
                last.then_inc(s["deg_full"], 1)

            def group(v, g, gg):
                pe.wait_ge(adjg_in[v], 16 * (gg + 1))
                for k in range(GT):
                    pe.wait_ge(s["u_free"], GT * g + k + 1)
                    held(pe)
                    row_tile(v, k, range(NT)).then_inc(s["u_full"], 1)
                    if k == 0:
                        degrees(v, g)

            pe.wait_ge(adjg_in[0], 16)
            pe.wait_ge(s["u_free"], GT)
            for b in range(NT // 8):
                pe.wait_ge(s["lo_made"], b + 1)
                for k in range(GT):
                    last = row_tile(0, k, range(8 * b, 8 * b + 8))
                    if b == NT // 8 - 1:
                        last.then_inc(s["u_full"], 1)
                        if k == 0:
                            degrees(0, 0)
            group(1, 1, 0)
            with pe.Fori(1, NG // 2) as gg:
                for v in range(2):
                    group(v, 2 * gg + v, gg)


def kernel(x, adj, L0_gnn_W, L0_gnn_V, L0_gnn_enc_bn_gamma, L0_gnn_enc_bn_beta, L0_gnn_enc_mlp_W,
           L0_gnn_enc_mlp_b, L0_gnn_enc_mlp_bn_gamma, L0_gnn_enc_mlp_bn_beta, L0_gnn_dec_mlp_W,
           L0_gnn_dec_mlp_b, L0_gnn_dec_mlp_bn_gamma, L0_gnn_dec_mlp_bn_beta):
    import numpy as np
    import concourse.bacc as bacc
    from concourse.bass_utils import run_bass_kernel_spmd

    x, adj, W = np.asarray(x), np.asarray(adj), np.asarray(L0_gnn_W)
    host = {
        "xT": x.T, "x": x, "adjT": adj.T, "W": W, "WT": W.transpose(0, 2, 1), "V": L0_gnn_V,
        "enc_g": L0_gnn_enc_bn_gamma, "enc_b": L0_gnn_enc_bn_beta,
        "encm_WT": np.asarray(L0_gnn_enc_mlp_W).T, "encm_bias": L0_gnn_enc_mlp_b,
        "encm_g": L0_gnn_enc_mlp_bn_gamma, "encm_b": L0_gnn_enc_mlp_bn_beta,
        "decm_WT": np.asarray(L0_gnn_dec_mlp_W).T, "decm_bias": L0_gnn_dec_mlp_b,
        "decm_g": L0_gnn_dec_mlp_bn_gamma, "decm_b": L0_gnn_dec_mlp_bn_beta,
    }
    nc = bacc.Bacc("TRN2", target_bir_lowering=False, num_devices=1)
    arrays, args = {}, []
    for name, a in host.items():
        a = np.ascontiguousarray(a)
        arrays[f"in_{name}"] = a
        args.append(nc.dram_tensor(f"in_{name}", a.shape, mybir.dt.from_np(a.dtype), kind="ExternalInput").ap())
    out = nc.dram_tensor("out", [N, F], F32, kind="ExternalOutput").ap()
    build(nc, *args, out)
    r = run_bass_kernel_spmd(nc, [arrays], core_ids=[0])
    return r.results[0]["out"]
```
